# Optimizing a Trainium2 kernel written in Bass

```python
import numpy as np
import jax
import jax.numpy as jnp

def _softmax(x, axis=-1):
    return jax.nn.softmax(x, axis=axis)

def _gelu(x):
    return jax.nn.gelu(x, approximate=True)

def _silu(x):
    return jax.nn.silu(x)

def _sigmoid(x):
    return jax.nn.sigmoid(x)

def _layernorm(x, axis=-1, eps=1e-05):
    m = jnp.mean(x, axis=axis, keepdims=True)
    v = jnp.var(x, axis=axis, keepdims=True)
    return (x - m) / jnp.sqrt(v + eps)

def _scatter_add(tgt, idx, src, axis=0):
    return tgt.at[idx].add(src)

def _segment_sum(src, seg, n):
    return jax.ops.segment_sum(src, seg, n)
kernel_name = 'mk_gnn_resnorm_d1_gnn_r8_bae1b1'

def setup_inputs(seed: int=0):
    np.random.seed(seed)
    _w = jnp.asarray

    def _rec_inputs():
        import jax
        import jax.numpy as jnp
        _gk = jax.random.key(seed)
        x = -0.000202 + 1 * jax.random.normal(jax.random.fold_in(_gk, 1), (6250, 128), jnp.float32)
        _s = jax.random.randint(jax.random.fold_in(_gk, 2), (50000,), 0, 6250, jnp.int32)
        _d = jax.random.randint(jax.random.fold_in(_gk, 3), (50000,), 0, 6250, jnp.int32)
        _loop = jnp.arange(6250, dtype=jnp.int32)
        src = jnp.concatenate([_s, _d, _loop])
        dst = jnp.concatenate([_d, _s, _loop])
        _o = jnp.argsort(dst, stable=True)
        src = src[_o]
        dst = dst[_o]
        edge_attr_96 = 5.93493e-05 + 1.00006 * jax.random.normal(jax.random.fold_in(_gk, 12), (106250, 96), jnp.float32)
        return (x, src, dst, edge_attr_96)
    x, src, dst, edge_attr_96 = _rec_inputs()

    def _L0_gnn_setup():
        import jax, jax.numpy as jnp
        import numpy as np
        N_NODES = 6250
        N_EDGES = 100000
        D_NODE_IN, D_EDGE, D_GRAPH = (128, 96, 64)
        HIDDEN, D_NODE_OUT = (256, 128)
        NUM_GRAPHS = 64
        BN_EPS = 1e-05
        key = jax.random.key(seed)
        ks = jax.random.split(key, 10)
        d_in = D_NODE_IN + D_EDGE + D_GRAPH
        return {'x': jax.random.normal(ks[0], (N_NODES, D_NODE_IN), jnp.float32), 'edge_index': jax.random.randint(ks[1], (2, N_EDGES), 0, N_NODES, jnp.int64), 'edge_attr': jax.random.normal(ks[2], (N_EDGES, D_EDGE), jnp.float32), 'u': jax.random.normal(ks[3], (NUM_GRAPHS, D_GRAPH), jnp.float32), 'batch': jnp.sort(jax.random.randint(ks[4], (N_NODES,), 0, NUM_GRAPHS, jnp.int64)), 'W1': jax.random.normal(ks[5], (d_in, HIDDEN), jnp.float32) / np.sqrt(d_in), 'b1': jnp.zeros((HIDDEN,), jnp.float32), 'gamma': jnp.ones((HIDDEN,), jnp.float32), 'beta': jnp.zeros((HIDDEN,), jnp.float32), 'W2': jax.random.normal(ks[6], (HIDDEN, D_NODE_OUT), jnp.float32) / np.sqrt(HIDDEN), 'b2': jnp.zeros((D_NODE_OUT,), jnp.float32)}
    _L0_gnn_all = _L0_gnn_setup()
    _L0_gnn_in = {k: v for k, v in _L0_gnn_all.items() if k in ('u', 'W1', 'b1', 'gamma', 'beta', 'W2', 'b2')}
    del _L0_gnn_all
    return {'x': x, 'src': src, 'dst': dst, 'edge_attr_96': edge_attr_96, 'L0_gnn_u': _L0_gnn_in['u'], 'L0_gnn_W1': _L0_gnn_in['W1'], 'L0_gnn_b1': _L0_gnn_in['b1'], 'L0_gnn_gamma': _L0_gnn_in['gamma'], 'L0_gnn_beta': _L0_gnn_in['beta'], 'L0_gnn_W2': _L0_gnn_in['W2'], 'L0_gnn_b2': _L0_gnn_in['b2']}

def reference(x, src, dst, edge_attr_96, L0_gnn_u, L0_gnn_W1, L0_gnn_b1, L0_gnn_gamma, L0_gnn_beta, L0_gnn_W2, L0_gnn_b2):
    import jax
    import jax.numpy as jnp

    def _L0_gnn_ref(x, edge_index, edge_attr, u, batch, W1, b1, gamma, beta, W2, b2):
        import jax, jax.numpy as jnp
        import numpy as np
        N_NODES = 6250
        N_EDGES = 100000
        D_NODE_IN, D_EDGE, D_GRAPH = (128, 96, 64)
        HIDDEN, D_NODE_OUT = (256, 128)
        NUM_GRAPHS = 64
        BN_EPS = 1e-05
        col = edge_index[1]
        n = x.shape[0]
        sums = jax.ops.segment_sum(edge_attr, col, num_segments=n)
        cnt = jax.ops.segment_sum(jnp.ones((edge_attr.shape[0], 1), edge_attr.dtype), col, num_segments=n)
        e_aggr = sums / jnp.maximum(cnt, 1.0)
        h = jnp.concatenate([x, e_aggr, u[batch]], axis=1)
        h = h @ W1 + b1
        mu = jnp.mean(h, axis=0)
        var = jnp.mean((h - mu) ** 2, axis=0)
        h = (h - mu) * jax.lax.rsqrt(var + BN_EPS) * gamma + beta
        h = jax.nn.relu(h)
        return h @ W2 + b2
    edge_index = jnp.stack([src, dst])
    batch0 = jnp.zeros((6250,), jnp.int32)
    x = _layernorm(x + _L0_gnn_ref(x, edge_index, edge_attr_96, L0_gnn_u, batch0, L0_gnn_W1, L0_gnn_b1, L0_gnn_gamma, L0_gnn_beta, L0_gnn_W2, L0_gnn_b2), axis=-1)
    return x

_drawn_inputs = setup_inputs


def setup_inputs(seed=0):
    import zlib

    import numpy as np

    out = dict(_drawn_inputs(seed))
    spreads = {'L0_gnn_b1': (0.0, 0.1),
     'L0_gnn_gamma': (1.0, 0.2),
     'L0_gnn_beta': (0.0, 0.1),
     'L0_gnn_b2': (0.0, 0.1)}
    factors = {}
    for name, (base, spread) in spreads.items():
        noise = np.random.default_rng([zlib.crc32(name.encode()), seed]).standard_normal(out[name].shape)
        drawn = base * np.exp(spread * noise) if base else spread * noise
        out[name] = jnp.asarray(drawn.astype(out[name].dtype))
    for name, factor in factors.items():
        out[name] = (out[name] * factor).astype(out[name].dtype)
    return out
```

```python
import numpy as np
import concourse.bass as bass
from concourse import mybir
from contextlib import ExitStack

N, DX, F, DU, HID = 6250, 128, 96, 64, 256
E = 106250
EPS = 1e-5
P = 128

SLOTS = 4
GE = P * SLOTS
NG = -(-E // GE)
TAIL_E = E - (NG - 1) * GE
W = 40
NPB = 512
Q = NPB // P
NB = N // NPB
LAST_N = N - NB * NPB
GPB = 17
STEP_GROUPS = NB * GPB
REST = NG - 1 - STEP_GROUPS
MARGIN = 6
PARTS = [(0, 5), (5, 9), (9, 13), (13, 17)]
LEAD = 4
CNT = F
R = F + 1
ACC_W = (NB + 1) * NPB
D_ROWS = [P, NG - P]
assert GPB * GE * NB * P <= E * P and E * NPB // N // GE == GPB
assert 0 <= REST < PARTS[0][1] and REST + 1 <= LEAD and ACC_W >= N + W


def bank_of(j):
    return j % 4 if j < 8 else (j - 8) % 3


def earlier_user(j):
    i = j - 1
    while bank_of(i % GPB) != bank_of(j):
        i -= 1
    return i


def lower_bounds():
    g = np.arange(2 * P)
    lb = np.where(g >= MARGIN, NPB * ((g - MARGIN) // GPB), 0)
    lb[NG:] = 0
    return np.ascontiguousarray(lb.reshape(2, P).T.astype(np.float32))


def gnn_kernel(nc, x, dst, edge, u, w1, b1, gamma, beta, w2, b2, lowest, out):
    fp32, bf16, i32 = mybir.dt.float32, mybir.dt.bfloat16, mybir.dt.int32
    ALU, ACT, AX = mybir.AluOpType, mybir.ActivationFunctionType, mybir.AxisListType
    ds = bass.ds

    with ExitStack() as ctx:
        def sb(name, shape, dt=fp32):
            return ctx.enter_context(nc.sbuf_tensor(name, shape, dt))

        def sem(name):
            return ctx.enter_context(nc.semaphore(name))

        ring = sb("ring", [P, GPB, SLOTS * F])
        tail = sb("tail", [P, SLOTS * F])
        onehot = sb("onehot", [P, GPB, SLOTS, W])
        acc = sb("acc", [R, ACC_W])
        acc_blk = sb("acc_blk", [R, Q, P])
        mean_nm = sb("mean_nm", [P, Q, F])
        meanT = sb("meanT", [F, NPB])
        x_blk = sb("x_blk", [P, Q, DX])
        x_last = sb("x_last", [P, DX])
        xT = sb("xT", [DX, NPB])
        xc = sb("xc", [P, (NB + 1) * Q, DX])
        x_mid = sb("x_mid", [P, Q, DX])
        x_junk = sb("x_junk", [P, Q, DX])
        x_mean = sb("x_mean", [P, Q])
        cnt1 = sb("cnt1", [P, Q])
        inv = sb("inv", [P, Q])
        hT = sb("hT", [P, 2, N])
        stats = sb("stats", [P, 2, NB + 1, 6])
        D = sb("D", [P, 2, GE], i32)
        Dl = sb("Dl", [P, 2, GE])
        dloc = sb("dloc", [P, NG, SLOTS])
        base = sb("base", [P, 2])
        span = sb("span", [P, 2])
        low = sb("low", [P, 2])
        bad = sb("bad", [P, 3, 2])
        base_row = sb("base_row", [1, NB + 1, 20], i32)
        flag = sb("flag", [1, 1], i32)
        iota = sb("iota", [P, NPB])
        ident = sb("ident", [P, P])
        ones = sb("ones", [P, 1])
        eps = sb("eps", [P, 1])
        cnt_w = sb("cnt_w", [P, P], bf16)
        w1x = sb("w1x", [DX, HID])
        w1e = sb("w1e", [F, HID])
        w1u = sb("w1u", [DU, HID])
        w2s = sb("w2s", [P, 2, DX])
        w2c = sb("w2c", [P, 2, DX])
        w2m = sb("w2m", [P, 2])
        vec_rows = sb("vec_rows", [7, P])
        vecs = sb("vecs", [P, 7])
        hb = sb("hb", [P, 2])
        b2s = sb("b2s", [P, DX])
        b2c = sb("b2c", [P, DX])
        b2m = sb("b2m", [P, 1])
        mv = sb("mv", [P, 2, 2])
        sd = sb("sd", [P, 2])
        rsd = sb("rsd", [P, 2])
        bn_s = sb("bn_s", [P, 2])
        bn_ms = sb("bn_ms", [P, 2])
        bn_t = sb("bn_t", [P, 2])
        rT = [sb(f"rT{k}", [P, 2, NPB]) for k in range(2)]
        y = [sb(f"y{k}", [P, Q, DX]) for k in range(2)]
        y_junk = [sb(f"y_junk{k}", [P, Q, DX]) for k in range(2)]
        ssq = [sb(f"ssq{k}", [P, Q]) for k in range(2)]
        ysd = [sb(f"ysd{k}", [P, Q]) for k in range(2)]
        yrs = [sb(f"yrs{k}", [P, Q]) for k in range(2)]
        yo = [sb(f"yo{k}", [P, Q, DX]) for k in range(2)]

        seg = [ctx.enter_context(nc.psum_tensor(f"seg{k}", [P, 512], fp32)) for k in range(4)]
        ps_xt = ctx.enter_context(nc.psum_tensor("ps_xt", [P, 512], fp32))
        ps_nm = ctx.enter_context(nc.psum_tensor("ps_nm", [P, 512], fp32))
        ps_h = [ctx.enter_context(nc.psum_tensor(f"ps_h{j}", [P, 512], fp32)) for j in range(2)]

        s_dst = [sem(f"s_dst{t}") for t in range(2)]
        s_low = sem("s_low")
        s_w = sem("s_w")
        s_tail = sem("s_tail")
        s_edge = [sem(f"s_edge{k}") for k in range(len(PARTS))]
        s_x = sem("s_x")
        s_xl = sem("s_xl")
        s_const = sem("s_const")
        s_tail0 = sem("s_tail0")
        s_acc0 = sem("s_acc0")
        s_pro = sem("s_pro")
        s_dl = sem("s_dl")
        s_dlT = sem("s_dlT")
        s_dcopy = sem("s_dcopy")
        s_dloc = sem("s_dloc")
        s_bad = sem("s_bad")
        s_rows = sem("s_rows")
        s_flag = sem("s_flag")
        s_vecT = sem("s_vecT")
        s_vecs = sem("s_vecs")
        s_hb = sem("s_hb")
        s_hbs = sem("s_hbs")
        s_w2 = sem("s_w2")
        s_b2c = sem("s_b2c")
        s_oh = sem("s_oh")
        s_seg = sem("s_seg")
        s_acc = sem("s_acc")
        s_final = sem("s_final")
        s_blk = sem("s_blk")
        s_nm = sem("s_nm")
        s_cnt = sem("s_cnt")
        s_inv = sem("s_inv")
        s_mean = sem("s_mean")
        s_mT = sem("s_mT")
        s_mTs = sem("s_mTs")
        s_xT = sem("s_xT")
        s_xTs = sem("s_xTs")
        s_xm = sem("s_xm")
        s_xmid = sem("s_xmid")
        s_xc = sem("s_xc")
        s_h = sem("s_h")
        s_hs = sem("s_hs")
        s_st = sem("s_st")
        s_mv = sem("s_mv")
        s_sd = sem("s_sd")
        s_bn = sem("s_bn")
        s_r = sem("s_r")
        s_y = sem("s_y")
        s_ys = sem("s_ys")
        s_sq = sem("s_sq")
        s_ysd = sem("s_ysd")
        s_yrs = sem("s_yrs")
        s_yo = sem("s_yo")
        s_out = [sem(f"s_out{k}") for k in range(2)]
        z_oh = sem("z_oh")
        z_seg = sem("z_seg")
        z_acc = sem("z_acc")
        z_sh = sem("z_sh")
        z_fill = sem("z_fill")

        ring_s = [[ring[:, j, s * F:(s + 1) * F] for s in range(SLOTS)] for j in range(GPB)]
        tail_s = [tail[:, s * F:(s + 1) * F] for s in range(SLOTS)]
        onehot_hi = onehot[:, :, :, :].rearrange("p g s w -> p (g s w)").bitcast(bf16)
        wide = onehot[:, :, :, :].rearrange("p g s w -> p (g s w)")[:, 0:SLOTS * NPB]
        wide_hi = wide.bitcast(bf16)

        def hi(j, s):
            a = 2 * (j * SLOTS + s) * W
            return onehot_hi[:, a + 1:a + 2 * W:2]

        edge_g = edge[0:(NG - 1) * GE, :].rearrange("(g p s) f -> p g (s f)", p=P, s=SLOTS)
        x_g = x[0:NB * NPB, :].rearrange("(b p q) f -> p b q f", p=P, q=Q)
        out_g = out[0:NB * NPB, :].rearrange("(b p q) f -> p b q f", p=P, q=Q)

        block = ctx.enter_context(nc.Block())

        def on_flag(eng):
            eng.wait_ge(s_flag, 1)
            return eng.value_load(flag[0:1, 0:1], min_val=0, max_val=1)

        @block.sync
        def _(sp):
            d0 = dst[0:P * GE].rearrange("(g e) -> g e", e=GE)
            sp.dma_start(D[:, 0, :], d0).then_inc(s_dst[0], 16)
            at, rows = P * GE, D_ROWS[1] - 1
            d1 = dst[at:at + rows * GE].rearrange("(g e) -> g e", e=GE)
            sp.dma_start(D[0:64, 1, :], d1[0:64, :]).then_inc(s_dst[1], 16)
            sp.dma_start(D[64:rows, 1, :], d1[64:rows, :]).then_inc(s_dst[1], 16)
            sp.dma_start(D[rows:rows + 1, 1, 0:TAIL_E], dst[E - TAIL_E:E].unsqueeze(0)).then_inc(s_dst[1], 16)
            sp.dma_start(D[rows:rows + 1, 1, TAIL_E:GE],
                         dst[E - (GE - TAIL_E):E].unsqueeze(0)).then_inc(s_dst[1], 16)

            def load_part(k, step):
                a, z = PARTS[k]
                src = edge_g[:, ds(step * GPB + a, z - a), :]
                sp.dma_start(ring[:, a:z, :], src).then_inc(s_edge[k], 16)

            def load_rest():
                src = edge_g[:, STEP_GROUPS:STEP_GROUPS + REST, :]
                sp.dma_start(ring[:, 0:REST, :], src).then_inc(s_edge[0], 16)

            def load_x(d):
                sp.wait_ge(s_xT, d)
                sp.wait_ge(s_xc, d)
                sp.dma_start(x_blk[:, :, :], x_g[:, ds(d, 1), :, :].rearrange("p b q f -> p (b q) f")).then_inc(s_x, 16)

            for k in range(len(PARTS)):
                load_part(k, 0)
            sp.dma_start(x_blk[:, :, :], x_g[:, 0, :, :]).then_inc(s_x, 16)
            sp.wait_ge(s_tail0, 2)
            rows = TAIL_E // SLOTS
            src = edge[E - TAIL_E:E - TAIL_E + rows * SLOTS, :].rearrange("(p s) f -> p (s f)", s=SLOTS)
            sp.dma_start(tail[0:rows, :], src).then_inc(s_tail, 16)
            more = TAIL_E - rows * SLOTS
            sp.dma_start(tail[rows:rows + 1, 0:more * F],
                         edge[E - more:E, :].rearrange("(p s) f -> p (s f)", s=more)).then_inc(s_tail, 16)
            sp.dma_start(x_last[0:LAST_N, :], x[NB * NPB:N, :]).then_inc(s_xl, 16)

            def next_step(b, x_too, last):
                for k, (a, z) in enumerate(PARTS):
                    sp.wait_ge(s_seg, b * GPB + z)
                    if not last:
                        load_part(k, b + 1)
                    elif k == 0:
                        load_rest()
                    if x_too and k == 2:
                        load_x(b)

            fl = on_flag(sp)
            with sp.If(fl == 0):
                next_step(0, False, False)
                with sp.Fori(1, NB - 1) as b:
                    next_step(b, True, False)
                next_step(NB - 1, True, True)
            with sp.Else():
                with sp.Fori(0, NB + 1) as k:
                    with sp.Fori(0, NB) as b:
                        done = k * NB + b
                        for part in range(1, len(PARTS)):
                            sp.wait_ge(s_edge[part], 16 * done + 16)
                        sp.wait_ge(s_edge[0], 16 * done + 16 * k + 16)
                        sp.wait_ge(z_seg, k * NG + b * GPB + 1)
                        for part in range(len(PARTS)):
                            load_part(part, b)
                    sp.wait_ge(z_seg, k * NG + STEP_GROUPS + 1)
                    load_rest()
                with sp.Fori(1, NB) as d:
                    load_x(d)

            def store(b, par):
                sp.wait_ge(s_yo, b + 3)
                sp.dma_start(out_g[:, ds(b, 1), :, :].rearrange("p b q f -> p (b q) f"),
                             yo[par][:, :, :]).then_inc(s_out[par], 16)

            store(0, 0)
            with sp.Fori(0, NB // 2 - 1) as i:
                store(2 * i + 1, 1)
                store(2 * i + 2, 0)
            store(NB - 1, 1)
            sp.wait_ge(s_yo, NB + 3)
            body = LAST_N - LAST_N % 16
            sp.dma_start(out[NB * NPB:NB * NPB + body, :], yo[0][0:body, 0, :]).then_inc(s_out[0], 16)
            sp.dma_start(out[NB * NPB + body:N, :], yo[0][body:LAST_N, 0, :]).then_inc(s_out[0], 16)
            sp.wait_ge(s_out[0], 16 * (NB // 2 + 3))
            sp.wait_ge(s_out[1], 16 * (NB // 2 + 1))

        @block.gpsimd
        def _(pool):
            pool.memset(ident[:, :], 0.0).then_inc(s_const, 1)
            pool.memset(ones[:, :], 1.0).then_inc(s_const, 1)
            pool.memset(eps[:, :], EPS).then_inc(s_const, 1)
            pool.wait_ge(s_const, 1)
            pool.affine_select(out=ident[:, :], in_=ident[:, :], compare_op=ALU.not_equal, fill=1.0, base=0,
                               pattern=[[-1, P]], channel_multiplier=1).then_inc(s_const, 1)
            pool.iota(iota[:, :], pattern=[[1, NPB]], base=0, channel_multiplier=0,
                      allow_small_or_imprecise_dtypes=True).then_inc(s_const, 1)
            pool.memset(vec_rows[:, :], 0.0).then_inc(s_tail0, 1)
            pool.memset(tail[:, :], 0.0).then_inc(s_tail0, 1)
            pool.memset(cnt_w[:, :], 0.0).then_inc(s_const, 1)
            pool.wait_ge(s_const, 6)
            pool.memset(cnt_w[:, CNT:CNT + 1], 1.0).then_inc(s_const, 1)
            pool.memset(acc[:, :], 0.0).then_inc(s_acc0, 1)
            pool.wait_ge(s_acc0, 1)
            pool.memset(acc_blk[:, :, :], 0.0).then_inc(s_nm, 1)

            def mask_last_group(n):
                pool.wait_ge(s_dcopy, 2 * n)
                pool.affine_select(out=dloc[:, NG - 1, :], in_=dloc[:, NG - 1, :], compare_op=ALU.is_gt,
                                   fill=-1.0, base=TAIL_E, pattern=[[-1, SLOTS]],
                                   channel_multiplier=-SLOTS).then_inc(s_dloc, 1)

            mask_last_group(1)
            fl = on_flag(pool)

            def copy_block(d):
                pool.wait_ge(s_nm, d + 1)
                pool.tensor_copy(acc_blk[:, :, :], acc[:, ds(d * NPB, NPB)].rearrange("r (p q) -> r q p", q=Q)
                                 ).then_inc(s_blk, 1)

            def centre(d, src, n, q, n_x):
                pool.wait_ge(s_xm, d + 1)
                if n_x is not None:
                    pool.wait_ge(s_x, n_x)
                else:
                    pool.wait_ge(s_xl, 16)
                mean = x_mean[0:n, 0:q].unsqueeze(2).broadcast_to([n, q, DX])
                pool.tensor_tensor(x_mid[0:n, 0:q, :], src, mean, ALU.subtract).then_inc(s_xmid, 1)
                pool.wait_ge(s_xmid, d + 1)
                pool.tensor_tensor(xc[0:n, ds(d * Q, q), :], x_mid[0:n, 0:q, :],
                                   b2c[0:n, :].unsqueeze(1).broadcast_to([n, q, DX]), ALU.add).then_inc(s_xc, 1)

            def dense(d):
                copy_block(d)
                centre(d, x_blk[:, :, :], P, Q, 16 * d + 16)

            pool.wait_ge(s_b2c, 1)
            with pool.If(fl == 0):
                with pool.Fori(0, NB - 1) as d:
                    pool.wait_ge(s_acc, (d + 1) * GPB + MARGIN + GPB)
                    dense(d)
            with pool.Else():
                pool.wait_ge(z_fill, 1)
                with pool.Fori(0, NB - 1) as d:
                    dense(d)
            pool.wait_ge(s_final, 1)
            dense(NB - 1)
            pool.wait_ge(s_nm, NB + 1)
            pool.tensor_copy(acc_blk[:, 0, 0:LAST_N], acc[:, NB * NPB:N]).then_inc(s_blk, 1)
            centre(NB, x_last[0:LAST_N, :].unsqueeze(1), LAST_N, 1, None)

            def scale(b, par, n, q):
                pool.wait_ge(s_yrs, b + 1)
                pool.wait_ge(s_out[par], 16 * ((b - par) // 2) + 16 if isinstance(b, int) else 8 * (b - par) + 16)
                rs = yrs[par][0:n, 0:q].unsqueeze(2).broadcast_to([n, q, DX])
                pool.tensor_tensor(yo[par][0:n, 0:q, :], y[par][0:n, 0:q, :], rs, ALU.mult).then_inc(s_yo, 1)

            scale(0, 0, P, Q)
            with pool.Fori(0, NB // 2 - 1) as i:
                for b, par in ((2 * i + 1, 1), (2 * i + 2, 0)):
                    pool.wait_ge(s_yrs, b + 1)
                    pool.wait_ge(s_out[par], 16 * i + 16 * (2 - par))
                    rs = yrs[par][:, :].unsqueeze(2).broadcast_to([P, Q, DX])
                    pool.tensor_tensor(yo[par][:, :, :], y[par][:, :, :], rs, ALU.mult).then_inc(s_yo, 1)
            scale(NB - 1, 1, P, Q)
            scale(NB, 0, LAST_N, 1)

        @block.scalar
        def _(act):
            act.dma_start(low[:, :], lowest).then_inc(s_low, 16)
            act.dma_start(w1x[:, :], w1[0:DX, :]).then_inc(s_w, 16)
            act.dma_start(w1e[:, :], w1[DX:DX + F, :]).then_inc(s_w, 16)
            act.dma_start(w1u[:, :], w1[DX + F:DX + F + DU, :]).then_inc(s_w, 16)
            act.dma_start(w2s[:, :, :], w2.rearrange("(j p) n -> p j n", j=2)).then_inc(s_w, 16)
            act.wait_ge(s_tail0, 2)
            act.dma_start(vec_rows[6:7, 0:DU], u[0:1, :]).then_inc(s_w, 16)
            for k, vec in enumerate((b1, gamma, beta)):
                act.dma_start(vec_rows[2 * k:2 * k + 2, :], vec.rearrange("(j p) -> j p", j=2)).then_inc(s_w, 16)
            act.dma_start(b2s[:, :], b2.unsqueeze(0).broadcast_to([P, DX])).then_inc(s_w, 16)
            fl = on_flag(act)

            def mean_x(d, src, n, q, n_x):
                if n_x is not None:
                    act.wait_ge(s_x, n_x)
                else:
                    act.wait_ge(s_xl, 16)
                    act.wait_ge(s_xc, NB)
                for k in range(q):
                    last = act.activation(x_junk[0:n, k, :], src[:, k, :], ACT.Identity, scale=1.0 / DX,
                                          accum_out=x_mean[0:n, k:k + 1])
                last.then_inc(s_xm, 1)

            def dense(d, last=False):
                n, q = (LAST_N, 1) if last else (P, Q)
                w = n * q
                if last:
                    mean_x(d, x_last[0:n, :].unsqueeze(1), n, q, None)
                else:
                    mean_x(d, x_blk[:, :, :], n, q, 16 * d + 16)
                act.wait_ge(s_xT, d + 1)
                act.activation(xT[:, 0:w], ps_xt[:, 0:w], ACT.Copy).then_inc(s_xTs, 1)
                act.wait_ge(s_inv, d + 1)
                for k in range(q):
                    ins = act.activation(mean_nm[0:n, k, :], ps_nm[0:n, k * P:k * P + F], ACT.Copy,
                                         scale=inv[0:n, k:k + 1])
                ins.then_inc(s_mean, 1)
                act.wait_ge(s_mT, d + 1)
                act.activation(meanT[:, 0:w], ps_xt[0:F, 0:w], ACT.Copy).then_inc(s_mTs, 1)
                for j in range(2):
                    act.wait_ge(s_h, 2 * d + j + 1)
                    act.activation(hT[:, j, ds(d * NPB, w)], ps_h[j][:, 0:w], ACT.Identity,
                                   bias=hb[:, j:j + 1]).then_inc(s_hs, 1)

            act.wait_ge(s_hbs, 2)
            with act.If(fl == 0):
                with act.Fori(0, NB - 1) as d:
                    dense(d)
            with act.Else():
                with act.Fori(0, NB - 1) as d:
                    dense(d)
            dense(NB - 1)
            dense(NB, last=True)

            act.wait_ge(s_mv, 2)
            act.activation(sd[:, :], mv[:, :, 1], ACT.Sqrt, bias=eps[:, 0:1]).then_inc(s_sd, 1)

            def relu(b, par, w):
                act.wait_ge(s_y, b + 1)
                for j in range(2):
                    act.activation(rT[par][:, j, 0:w], hT[:, j, ds(b * NPB, w)], ACT.Relu,
                                   bias=bn_t[:, j:j + 1], scale=bn_s[:, j:j + 1]).then_inc(s_r, 1)

            def root(b, par, n, q):
                act.wait_ge(s_sq, b + 1)
                act.activation(ysd[par][0:n, 0:q], ssq[par][0:n, 0:q], ACT.Sqrt, bias=eps[0:n, 0:1],
                               scale=1.0 / DX).then_inc(s_ysd, 1)

            act.wait_ge(s_bn, 4)
            relu(0, 0, NPB)
            with act.Fori(0, NB // 2 - 1) as i:
                relu(2 * i + 1, 1, NPB)
                root(2 * i, 0, P, Q)
                relu(2 * i + 2, 0, NPB)
                root(2 * i + 1, 1, P, Q)
            relu(NB - 1, 1, NPB)
            root(NB - 2, 0, P, Q)
            relu(NB, 0, LAST_N)
            root(NB - 1, 1, P, Q)
            root(NB, 0, LAST_N, 1)

        @block.tensor
        def _(pe):
            pe.wait_ge(s_const, 4)

            def transpose_dst(n):
                for t, rows in enumerate(D_ROWS):
                    pe.wait_ge(s_dl, 2 * n - 1 + t)
                    for s in range(SLOTS):
                        ins = pe.transpose(seg[t][:, s * P:s * P + rows], Dl[0:rows, t, s::SLOTS],
                                           ident[0:rows, 0:rows])
                    ins.then_inc(s_dlT, 1)

            pe.wait_ge(s_bad, 1)
            pe.matmul(seg[2][0:1, 0:P], base[:, 0:1], ident[:, :], start=True, stop=True)
            pe.matmul(seg[2][0:1, P:NG], base[0:D_ROWS[1], 1:2], ident[0:D_ROWS[1], 0:D_ROWS[1]], start=True, stop=True)
            pe.matmul(seg[2][0:1, 2 * P:2 * P + 2], ones[:, :], bad[:, 2, :], start=True, stop=True).then_inc(s_rows, 1)
            transpose_dst(1)
            pe.wait_ge(s_w, 16 * 9)
            pe.transpose(ps_nm[:, 0:7], vec_rows[:, :], ident[0:7, 0:7]).then_inc(s_vecT, 1)
            pe.wait_ge(s_vecs, 1)
            for j in range(2):
                ins = pe.matmul(seg[3][:, j:j + 1], w1u[:, j * P:(j + 1) * P], vecs[0:DU, 6:7], start=True, stop=True)
            ins.then_inc(s_hb, 1)
            fl = on_flag(pe)

            def sum_group(ps, rows, onehots, onehots_hi, done):
                pe.matmul(ps, cnt_w[:, :], onehots_hi[0], start=True, stop=False)
                for s in range(SLOTS):
                    pe.matmul(ps[0:F, :], rows[s], onehots[s], start=False, stop=False)
                for s in range(1, SLOTS):
                    ins = pe.matmul(ps, cnt_w[:, :], onehots_hi[s], start=False, stop=s == SLOTS - 1)
                ins.then_inc(done, 1)

            def transpose_x(d, last=False):
                if last:
                    pe.wait_ge(s_xl, 16)
                    pe.wait_ge(s_mTs, NB)
                    pe.transpose(ps_xt[:, 0:LAST_N], x_last[0:LAST_N, :], ident[0:LAST_N, 0:LAST_N]).then_inc(s_xT, 1)
                else:
                    pe.wait_ge(s_x, 16 * d + 16)
                    for q in range(Q):
                        ins = pe.transpose(ps_xt[:, q * P:(q + 1) * P], x_blk[:, q, :], ident[:, :])
                    ins.then_inc(s_xT, 1)

            def to_nodes(d, last=False):
                n, q = (LAST_N, 1) if last else (P, Q)
                pe.wait_ge(s_blk, d + 1)
                for k in range(q):
                    ins = pe.transpose(ps_nm[0:n, k * P:k * P + R], acc_blk[:, k, 0:n], ident[0:R, 0:R])
                ins.then_inc(s_nm, 1)

            def to_features(d, last=False):
                n, q = (LAST_N, 1) if last else (P, Q)
                pe.wait_ge(s_xTs, d + 1)
                pe.wait_ge(s_mean, d + 1)
                for k in range(q):
                    ins = pe.transpose(ps_xt[0:F, k * n:(k + 1) * n], mean_nm[0:n, k, :], ident[0:n, 0:n])
                ins.then_inc(s_mT, 1)

            def hidden(d, j, w=NPB):
                if j == 0:
                    pe.wait_ge(s_mTs, d + 1)
                pe.matmul(ps_h[j][:, 0:w], w1x[:, j * P:(j + 1) * P], xT[:, 0:w], start=True, stop=False)
                pe.matmul(ps_h[j][:, 0:w], w1e[:, j * P:(j + 1) * P], meanT[:, 0:w], start=False,
                          stop=True).then_inc(s_h, 1)

            def group(b, j, rows):
                pe.wait_ge(s_oh, b * GPB + j + 1)
                pe.wait_ge(s_acc, b * GPB + earlier_user(j) + 1 + GPB)
                sum_group(seg[bank_of(j)][:, 0:W], rows, [onehot[:, j, s, :] for s in range(SLOTS)],
                          [hi(j, s) for s in range(SLOTS)], s_seg)

            def step(b, dense):
                starts = {a: k for k, (a, _) in enumerate(PARTS)}
                for j in range(GPB):
                    if j in starts:
                        pe.wait_ge(s_edge[starts[j]], 16 * b + 16)
                    group(b, j, ring_s[j])
                    if dense and j == 1:
                        transpose_x(b - 1)
                    if dense and j == MARGIN + 2:
                        to_nodes(b - 1)
                    if dense and j == MARGIN + 5:
                        to_features(b - 1)
                    if dense and j == MARGIN + 7:
                        hidden(b - 1, 0)
                    if dense and j == MARGIN + 9:
                        hidden(b - 1, 1)

            with pe.If(fl == 0):
                step(0, False)
                with pe.Fori(1, NB) as b:
                    step(b, True)
                pe.wait_ge(s_edge[0], 16 * NB + 16)
                for j in range(REST):
                    group(NB, j, ring_s[j])
                pe.wait_ge(s_tail, 32)
                group(NB, REST, tail_s)
            with pe.Else():
                transpose_dst(2)

                def slow_group(n, rows):
                    pe.wait_ge(z_oh, n + 1)
                    sum_group(seg[3][:, :], rows, [wide[:, s * NPB:(s + 1) * NPB] for s in range(SLOTS)],
                              [wide_hi[:, 2 * s * NPB + 1:2 * (s + 1) * NPB:2] for s in range(SLOTS)], z_seg)

                pe.wait_ge(s_tail, 32)
                with pe.Fori(0, NB + 1) as k:
                    with pe.Fori(0, NB) as b:
                        for part in range(1, len(PARTS)):
                            pe.wait_ge(s_edge[part], 16 * (k * NB + b) + 32)
                        pe.wait_ge(s_edge[0], 16 * (k * NB + b) + 16 * k + 32)
                        for j in range(GPB):
                            slow_group(k * NG + b * GPB + j, ring_s[j])
                    pe.wait_ge(s_edge[0], 16 * (k * NB + NB) + 16 * k + 32)
                    for j in range(REST):
                        slow_group(k * NG + STEP_GROUPS + j, ring_s[j])
                    slow_group(k * NG + NG - 1, tail_s)
                with pe.Fori(0, NB - 1) as d:
                    transpose_x(d)
                    to_nodes(d)
                    to_features(d)
                    hidden(d, 0)
                    hidden(d, 1)
            transpose_x(NB - 1)
            to_nodes(NB - 1)
            to_features(NB - 1)
            hidden(NB - 1, 0)
            hidden(NB - 1, 1)
            transpose_x(NB, last=True)
            to_nodes(NB, last=True)
            to_features(NB, last=True)
            pe.wait_ge(s_hs, 2 * NB)
            hidden(NB, 0, LAST_N)
            hidden(NB, 1, LAST_N)

            def second(b, par, n, q):
                pe.wait_ge(s_r, 2 * b + 2)
                pe.wait_ge(s_ys, b + 1)
                for k in range(q):
                    for j in range(2):
                        ins = pe.matmul(seg[par][0:n, k * DX:(k + 1) * DX], rT[par][:, j, k * n:(k + 1) * n],
                                        w2c[:, j, :], start=j == 0, stop=j == 1)
                ins.then_inc(s_y, 1)

            pe.wait_ge(s_w2, 2)
            second(0, 0, P, Q)
            with pe.Fori(0, NB // 2 - 1) as i:
                second(2 * i + 1, 1, P, Q)
                second(2 * i + 2, 0, P, Q)
            second(NB - 1, 1, P, Q)
            second(NB, 0, LAST_N, 1)

        @block.vector
        def _(dve):
            pro = [0]

            def own(ins):
                pro[0] += 1
                ins.then_inc(s_pro, 1)
                dve.wait_ge(s_pro, pro[0])

            dve.memset(base[:, :], 0.0)
            own(dve.memset(span[:, :], 0.0))
            for t, rows in enumerate(D_ROWS):
                dve.wait_ge(s_dst[t], 16 if t == 0 else 64)
                own(dve.tensor_reduce(base[0:rows, t:t + 1], D[0:rows, t, :], AX.X, ALU.min))
                dve.tensor_scalar(Dl[0:rows, t, :], D[0:rows, t, :], base[0:rows, t:t + 1], None,
                                  ALU.subtract).then_inc(s_dl, 1)
                dve.wait_ge(s_dl, t + 1)
                own(dve.tensor_reduce(span[0:rows, t:t + 1], Dl[0:rows, t, :], AX.X, ALU.max))
            dve.wait_ge(s_low, 16)
            dve.tensor_tensor(bad[:, 0, :], base[:, :], low[:, :], ALU.is_lt)
            own(dve.tensor_scalar(bad[:, 1, :], span[:, :], float(W), None, ALU.is_ge))
            own(dve.scalar_tensor_tensor(bad[:, 1, :], base[:, :], float(N), bad[:, 1, :], ALU.is_ge, ALU.add))
            dve.tensor_tensor(bad[:, 2, :], bad[:, 0, :], bad[:, 1, :], ALU.add).then_inc(s_bad, 1)
            dve.wait_ge(s_rows, 1)
            dve.tensor_scalar(base_row[0:1, 0:NB, 0:GPB],
                              seg[2][0:1, 0:STEP_GROUPS].rearrange("o (b g) -> o b g", g=GPB),
                              0.0, float(N - 1), ALU.max, ALU.min)
            own(dve.tensor_scalar(base_row[0:1, NB, 0:REST + 1], seg[2][0:1, STEP_GROUPS:NG],
                                  0.0, float(N - 1), ALU.max, ALU.min))
            own(dve.tensor_reduce(x_mean[0:1, 0:1], seg[2][0:1, 2 * P:2 * P + 2], AX.X, ALU.add))
            dve.tensor_scalar(flag[0:1, 0:1], x_mean[0:1, 0:1], 0.5, None, ALU.is_ge).then_inc(s_flag, 1)

            def take_dst(n):
                for t, rows in enumerate(D_ROWS):
                    dve.wait_ge(s_dlT, 2 * n - 1 + t)
                    dve.tensor_copy(dloc[:, t * P:t * P + rows, :].rearrange("p g s -> p s g"),
                                    seg[t][:, :].rearrange("p (s g) -> p s g", g=P)[:, :, 0:rows]).then_inc(s_dcopy, 1)

            take_dst(1)
            dve.wait_ge(s_w, 16 * 9)
            dve.wait_ge(s_vecT, 1)
            dve.tensor_copy(vecs[:, :], ps_nm[:, 0:7]).then_inc(s_vecs, 1)
            dve.wait_ge(s_vecs, 1)
            dve.wait_ge(s_hb, 1)
            dve.tensor_tensor(hb[:, :], seg[3][:, 0:2], vecs[:, 0:2], ALU.add).then_inc(s_hbs, 2)
            dve.tensor_reduce(b2m[:, :], b2s[:, :], AX.X, ALU.add)
            own(dve.tensor_reduce(w2m[:, :], w2s[:, :, :], AX.X, ALU.add))
            own(dve.tensor_scalar(b2m[:, :], b2m[:, :], 1.0 / DX, None, ALU.mult))
            own(dve.tensor_scalar(w2m[:, :], w2m[:, :], 1.0 / DX, None, ALU.mult))
            dve.tensor_scalar(b2c[:, :], b2s[:, :], b2m[:, 0:1], None, ALU.subtract).then_inc(s_b2c, 1)
            for j in range(2):
                dve.tensor_scalar(w2c[:, j, :], w2s[:, j, :], w2m[:, j:j + 1], None, ALU.subtract).then_inc(s_w2, 1)
            dve.wait_ge(s_dloc, 1)
            dve.wait_ge(s_acc0, 1)
            fl = on_flag(dve)

            def inverse(d, last=False):
                n, q = (LAST_N, 1) if last else (P, Q)
                dve.wait_ge(s_nm, d + 2)
                counts = ps_nm[0:n, :].rearrange("p (q f) -> p q f", f=P)[:, 0:q, CNT]
                dve.tensor_scalar(cnt1[0:n, 0:q], counts, 1.0, None, ALU.max).then_inc(s_cnt, 1)
                dve.wait_ge(s_cnt, d + 1)
                dve.reciprocal(inv[0:n, 0:q], cnt1[0:n, 0:q]).then_inc(s_inv, 1)

            def statistics(d, w=NPB):
                for j in range(2):
                    dve.wait_ge(s_hs, 2 * d + j + 1)
                    dve.bn_stats(stats[:, j, ds(d, 1), :].rearrange("p b k -> p (b k)"),
                                 hT[:, j, ds(d * NPB, w)]).then_inc(s_st, 1)

            def one_hot(b, j):
                group = b * GPB + j
                where = dloc[:, ds(group, 1), :].rearrange("p g s -> p (g s)").unsqueeze(2).broadcast_to([P, SLOTS, W])
                nodes = iota[:, 0:W].unsqueeze(1).broadcast_to([P, SLOTS, W])
                dve.tensor_tensor(onehot[:, j % GPB, :, :], nodes, where, ALU.is_equal).then_inc(s_oh, 1)

            def bases(b, n):
                row = base_row[0:1, ds(b, 1), 0:n].rearrange("o b g -> o (b g)")
                _, vals = nc.values_load_multi_w_load_instructions(
                    row, engines=[mybir.EngineType.DVE], min_val=0, max_val=N - 1,
                    skip_runtime_bounds_check_because="base_row is clamped to these bounds when it is written")
                return vals

            def add_group(b, j, at, final=False):
                dve.wait_ge(s_seg, b * GPB + j + 1)
                dve.wait_ge(s_acc, b * GPB + j + GPB)
                window = acc[:, ds(at, W)]
                ins = dve.tensor_tensor(window, window, seg[bank_of(j)][0:R, 0:W], ALU.add)
                ins.then_inc(s_final if final else s_acc, 1)

            def step(b, dense):
                at = bases(b, GPB)
                for j in range(GPB):
                    one_hot(b, j + LEAD)
                    add_group(b, j, at[j])
                    if dense and j == MARGIN + 2:
                        inverse(b - 1)
                if dense:
                    statistics(b - 1)

            with dve.If(fl == 0):
                dve.memset(cnt1[:, :], 0.0).then_inc(s_acc, GPB)
                for j in range(LEAD):
                    one_hot(0, j)
                step(0, False)
                with dve.Fori(1, NB) as b:
                    step(b, True)
                at = bases(NB, REST + 1)
                for j in range(REST + 1):
                    add_group(NB, j, at[j], final=j == REST)
            with dve.Else():
                for t, rows in enumerate(D_ROWS):
                    dve.tensor_copy(Dl[0:rows, t, :], D[0:rows, t, :]).then_inc(s_dl, 1)
                take_dst(2)
                dve.wait_ge(s_dloc, 2)
                flat = dloc[:, :, :].rearrange("p g s -> p (g s)")

                def slow_group(k, g):
                    n = k * NG + g
                    for s in range(SLOTS):
                        ins = dve.tensor_scalar(wide[:, s * NPB:(s + 1) * NPB], iota[:, :],
                                                flat[:, ds(g * SLOTS + s, 1)], None, ALU.is_equal)
                    ins.then_inc(z_oh, 1)
                    dve.wait_ge(z_seg, n + 2)
                    cols = acc[:, ds(k * NPB, NPB)]
                    dve.tensor_tensor(cols, cols, seg[3][0:R, :], ALU.add).then_inc(z_acc, 1)
                    dve.wait_ge(z_acc, n + 1)

                dve.memset(cnt1[:, :], 0.0).then_inc(z_seg, 1)
                with dve.Fori(0, NB + 1) as k:
                    with dve.Fori(0, NG) as g:
                        slow_group(k, g)
                    dve.tensor_scalar(flat, flat, float(NPB), None, ALU.subtract).then_inc(z_sh, 1)
                    dve.wait_ge(z_sh, k + 1)
                dve.memset(cnt1[:, :], 0.0).then_inc(z_fill, 1)
                with dve.Fori(0, NB - 1) as d:
                    inverse(d)
                    statistics(d)
                dve.memset(cnt1[:, :], 0.0).then_inc(s_final, 1)
            inverse(NB - 1)
            statistics(NB - 1)
            inverse(NB, last=True)
            statistics(NB, LAST_N)

            dve.wait_ge(s_st, 2 * (NB + 1))
            for j in range(2):
                dve.bn_aggr(mv[:, j, :], stats[:, j, :, :].rearrange("p b k -> p (b k)")).then_inc(s_mv, 1)
            dve.wait_ge(s_mv, 2)
            dve.wait_ge(s_sd, 1)
            dve.reciprocal(rsd[:, :], sd[:, :]).then_inc(s_bn, 1)
            dve.wait_ge(s_bn, 1)
            dve.tensor_tensor(bn_s[:, :], rsd[:, :], vecs[:, 2:4], ALU.mult).then_inc(s_bn, 1)
            dve.wait_ge(s_bn, 2)
            dve.tensor_tensor(bn_ms[:, :], mv[:, :, 0], bn_s[:, :], ALU.mult).then_inc(s_bn, 1)
            dve.wait_ge(s_bn, 3)
            dve.tensor_tensor(bn_t[:, :], vecs[:, 4:6], bn_ms[:, :], ALU.subtract).then_inc(s_bn, 1)
            dve.memset(yrs[0][:, :], 0.0).then_inc(s_y, 2)
            dve.memset(yrs[1][:, :], 0.0).then_inc(s_ys, 2)
            dve.memset(ysd[0][:, :], 0.0).then_inc(s_yo, 2)
            dve.memset(ysd[1][:, :], 0.0).then_inc(s_out[0], 16)
            dve.memset(ssq[1][:, :], 0.0).then_inc(s_out[1], 16)

            def finish(b, par, n, q):
                dve.wait_ge(s_y, b + 3)
                dve.wait_ge(s_yo, b + 1)
                dve.tensor_tensor(y[par][0:n, 0:q, :],
                                  seg[par][0:n, 0:q * DX].rearrange("p (q f) -> p q f", q=q),
                                  xc[0:n, ds(b * Q, q), :], ALU.add).then_inc(s_ys, 1)
                dve.wait_ge(s_ys, b + 3)
                for k in range(q):
                    ins = dve.tensor_tensor_reduce(out=y_junk[par][0:n, k, :], in0=y[par][0:n, k, :],
                                                   in1=y[par][0:n, k, :], scale=1.0, scalar=0.0, op0=ALU.mult,
                                                   op1=ALU.add, accum_out=ssq[par][0:n, k:k + 1])
                ins.then_inc(s_sq, 1)

            def inverse_sd(b, par, n, q):
                dve.wait_ge(s_ysd, b + 1)
                dve.reciprocal(yrs[par][0:n, 0:q], ysd[par][0:n, 0:q]).then_inc(s_yrs, 1)

            dve.wait_ge(s_xc, NB + 1)
            finish(0, 0, P, Q)
            with dve.Fori(0, NB // 2 - 1) as i:
                finish(2 * i + 1, 1, P, Q)
                inverse_sd(2 * i, 0, P, Q)
                finish(2 * i + 2, 0, P, Q)
                inverse_sd(2 * i + 1, 1, P, Q)
            finish(NB - 1, 1, P, Q)
            inverse_sd(NB - 2, 0, P, Q)
            finish(NB, 0, LAST_N, 1)
            inverse_sd(NB - 1, 1, P, Q)
            inverse_sd(NB, 0, LAST_N, 1)


def kernel(x, src, dst, edge_attr_96, L0_gnn_u, L0_gnn_W1, L0_gnn_b1, L0_gnn_gamma, L0_gnn_beta, L0_gnn_W2,
           L0_gnn_b2):
    import concourse.bacc as _bacc
    from concourse import mybir as _mybir
    from concourse.bass_utils import run_bass_kernel_spmd as _run

    nc = _bacc.Bacc("TRN2", target_bir_lowering=False, num_devices=1)
    arrays, args = {}, []
    for name, a in (("x", x), ("dst", dst), ("edge", edge_attr_96), ("u", L0_gnn_u), ("w1", L0_gnn_W1),
                    ("b1", L0_gnn_b1), ("gamma", L0_gnn_gamma), ("beta", L0_gnn_beta), ("w2", L0_gnn_W2),
                    ("b2", L0_gnn_b2), ("lowest", lower_bounds())):
        a = np.ascontiguousarray(a)
        arrays[f"in_{name}"] = a
        args.append(nc.dram_tensor(f"in_{name}", a.shape, _mybir.dt.from_np(a.dtype), kind="ExternalInput").ap())
    args.append(nc.dram_tensor("out_0", (N, DX), _mybir.dt.float32, kind="ExternalOutput").ap())
    gnn_kernel(nc, *args)
    r = _run(nc, [arrays], core_ids=[0])
    return r.results[0]["out_0"]
```

```python
import numpy as np
import concourse.bass as bass
from concourse import mybir
from contextlib import ExitStack

N, DX, F, DU, HID = 6250, 128, 96, 64, 256
E = 106250
EPS = 1e-5
P = 128

SLOTS = 4
GE = P * SLOTS
NG = -(-E // GE)
W = 56
NPB = 512
Q = NPB // P
NB = N // NPB
LAST_N = N - NB * NPB
GPB = 17
STEP_GROUPS = NB * GPB
REST = NG - STEP_GROUPS
MARGIN = 6
PARTS = [(0, 5), (5, 9), (9, 13), (13, 17)]
YS = 4
LAG = 2
LEAD = 4
R = F + 1
CNT = F
ACC_W = (NB + 1) * NPB
PAIRS = NG // 2
assert GPB * GE * NB * P <= E * P and E * NPB // N // GE == GPB
assert NG == 2 * PAIRS and 0 < REST <= min(PARTS[0][1], LEAD) and ACC_W >= N + W


def bank_of(j):
    return j % 4 if j < 8 else (j - 8) % 3


def earlier_user(j):
    i = j - 1
    while bank_of(i % GPB) != bank_of(j):
        i -= 1
    return i


def last_stage(eng, do):
    for b in range(LAG):
        do(b, b % YS, b % 2, P, Q)
    turns = (NB - LAG) // YS
    with eng.Fori(0, turns) as i:
        for k in range(LAG, LAG + YS):
            do(i * YS + k, k % YS, k % 2, P, Q)
    for b in range(LAG + turns * YS, NB):
        do(b, b % YS, b % 2, P, Q)
    do(NB, NB % YS, NB % 2, LAST_N, 1)


def lagging(b, buf, do):
    if not isinstance(b, int) or b >= LAG:
        do(b - LAG, (buf - LAG) % YS, P, Q)


def flush(do):
    for b in range(NB + 1 - LAG, NB):
        do(b, b % YS, P, Q)
    do(NB, NB % YS, LAST_N, 1)


def lower_bounds():
    g = np.arange(NG)
    return np.where(g >= MARGIN, NPB * ((g - MARGIN) // GPB), 0).reshape(PAIRS, 2).astype(np.float32)


def gnn_kernel(nc, x, xt, dst_rows, dst_cols, edge, u, w1, b1, gamma, beta, w2, b2, lowest, out):
    fp32, bf16, i32 = mybir.dt.float32, mybir.dt.bfloat16, mybir.dt.int32
    ALU, ACT, AX = mybir.AluOpType, mybir.ActivationFunctionType, mybir.AxisListType
    ds = bass.ds

    with ExitStack() as ctx:
        def sb(name, shape, dt=fp32):
            return ctx.enter_context(nc.sbuf_tensor(name, shape, dt))

        def sem(name):
            return ctx.enter_context(nc.semaphore(name))

        ring = sb("ring", [P, GPB, SLOTS * R])
        onehot = sb("onehot", [P, GPB, SLOTS, W])
        acc = sb("acc", [R, ACC_W])
        acc_blk = sb("acc_blk", [R, Q, P])
        mean_nm = sb("mean_nm", [P, Q, F])
        meanT = sb("meanT", [F, NPB])
        x_blk = sb("x_blk", [P, Q, DX])
        x_last = sb("x_last", [P, DX])
        xT = sb("xT", [DX, NPB])
        xT_last = sb("xT_last", [DX, LAST_N])
        xc = sb("xc", [P, (NB + 1) * Q, DX])
        x_mid = sb("x_mid", [P, Q, DX])
        x_junk = sb("x_junk", [P, Q, DX])
        x_mean = sb("x_mean", [P, Q])
        cnt1 = sb("cnt1", [P, Q])
        inv = sb("inv", [P, Q])
        hT = sb("hT", [P, 2, N])
        stats = sb("stats", [P, 2, NB + 1, 6])
        D = sb("D", [PAIRS, 2, GE], i32)
        dcols = sb("dcols", [P, NG, SLOTS], i32)
        dloc = sb("dloc", [P, NG, SLOTS])
        base = sb("base", [PAIRS, 2])
        most = sb("most", [PAIRS, 2])
        span = sb("span", [PAIRS, 2])
        low = sb("low", [PAIRS, 2])
        bad = sb("bad", [PAIRS, 3, 2])
        base_row = sb("base_row", [1, NB + 1, 20], i32)
        flag = sb("flag", [1, 1], i32)
        iota = sb("iota", [P, NPB])
        ident = sb("ident", [P, P])
        ones = sb("ones", [P, 1])
        eps = sb("eps", [P, 1])
        w1x = sb("w1x", [DX, HID])
        w1e = sb("w1e", [F, HID])
        w1u = sb("w1u", [DU, HID])
        w2s = sb("w2s", [P, 2, DX])
        w2c = sb("w2c", [P, 2, DX])
        w2m = sb("w2m", [P, 2])
        vec_rows = sb("vec_rows", [7, P])
        vecs = sb("vecs", [P, 7])
        hb = sb("hb", [P, 2])
        b2s = sb("b2s", [P, DX])
        b2c = sb("b2c", [P, DX])
        b2m = sb("b2m", [P, 1])
        mv = sb("mv", [P, 2, 2])
        sd = sb("sd", [P, 2])
        rsd = sb("rsd", [P, 2])
        bn_s = sb("bn_s", [P, 2])
        bn_ms = sb("bn_ms", [P, 2])
        bn_t = sb("bn_t", [P, 2])
        rT = [sb(f"rT{k}", [P, 2, NPB]) for k in range(2)]
        y = [sb(f"y{k}", [P, Q, DX]) for k in range(YS)]
        y_sq = [sb(f"y_sq{k}", [P, Q, DX]) for k in range(YS)]
        ssq = [sb(f"ssq{k}", [P, Q]) for k in range(YS)]
        ysd = [sb(f"ysd{k}", [P, Q]) for k in range(YS)]
        yrs = [sb(f"yrs{k}", [P, Q]) for k in range(YS)]
        warm = sb("warm", [P, NPB], bf16)
        spare = sb("spare", [P, 10])
        act_spare = sb("act_spare", [P, 1])

        seg = [ctx.enter_context(nc.psum_tensor(f"seg{k}", [P, 512], fp32)) for k in range(4)]
        ps_ft = ctx.enter_context(nc.psum_tensor("ps_ft", [P, 512], fp32))
        ps_nm = ctx.enter_context(nc.psum_tensor("ps_nm", [P, 512], fp32))
        ps_h = [ctx.enter_context(nc.psum_tensor(f"ps_h{j}", [P, 512], fp32)) for j in range(2)]

        s_dst = sem("s_dst")
        s_dcol = sem("s_dcol")
        s_low = sem("s_low")
        s_w = sem("s_w")
        s_edge = [sem(f"s_edge{k}") for k in range(len(PARTS))]
        s_x = sem("s_x")
        s_xl = sem("s_xl")
        s_const = sem("s_const")
        s_vec0 = sem("s_vec0")
        s_warm = sem("s_warm")
        s_table = sem("s_table")
        s_acc0 = sem("s_acc0")
        s_pro = sem("s_pro")
        s_dloc = sem("s_dloc")
        s_base = sem("s_base")
        s_brow = sem("s_brow")
        s_rows = sem("s_rows")
        s_bad = sem("s_bad")
        s_nbad = sem("s_nbad")
        s_flag = sem("s_flag")
        s_vecT = sem("s_vecT")
        s_vecs = sem("s_vecs")
        s_small = sem("s_small")
        s_hb = sem("s_hb")
        s_hbs = sem("s_hbs")
        s_w2 = sem("s_w2")
        s_b2c = sem("s_b2c")
        s_oh = sem("s_oh")
        s_seg = sem("s_seg")
        s_acc = sem("s_acc")
        s_final = sem("s_final")
        s_blk = sem("s_blk")
        s_nm = sem("s_nm")
        s_cnt = sem("s_cnt")
        s_inv = sem("s_inv")
        s_mean = sem("s_mean")
        s_mT = sem("s_mT")
        s_mTs = sem("s_mTs")
        s_xT = sem("s_xT")
        s_xm = sem("s_xm")
        s_xmid = sem("s_xmid")
        s_xc = sem("s_xc")
        s_h = sem("s_h")
        s_hs = sem("s_hs")
        s_st = sem("s_st")
        s_mv = sem("s_mv")
        s_sd = sem("s_sd")
        s_bn = sem("s_bn")
        s_r = sem("s_r")
        s_y = sem("s_y")
        s_ys = sem("s_ys")
        s_sq = sem("s_sq")
        s_ysd = sem("s_ysd")
        s_yrs = sem("s_yrs")
        s_yo = sem("s_yo")
        s_out = sem("s_out")
        z_oh = sem("z_oh")
        z_seg = sem("z_seg")
        z_acc = sem("z_acc")
        z_sh = sem("z_sh")
        z_fill = sem("z_fill")

        ring_s = [[ring[:, j, s * R:(s + 1) * R] for s in range(SLOTS)] for j in range(GPB)]
        wide = onehot[:, :, :, :].rearrange("p g s w -> p (g s w)")[:, 0:SLOTS * NPB]

        edge_g = edge.rearrange("(g p s) f -> p g (s f)", p=P, s=SLOTS)
        x_g = x[0:NB * NPB, :].rearrange("(b p q) f -> p b q f", p=P, q=Q)
        out_g = out[0:NB * NPB, :].rearrange("(b p q) f -> p b q f", p=P, q=Q)

        block = ctx.enter_context(nc.Block())

        def on_flag(eng):
            eng.wait_ge(s_flag, 1)
            return eng.value_load(flag[0:1, 0:1], min_val=0, max_val=1)

        @block.sync
        def _(sp):
            sp.dma_start(D[:, :, :], dst_rows).then_inc(s_dst, 16)
            sp.dma_start(low[:, :], lowest).then_inc(s_low, 16)
            sp.dma_start(dcols[:, :, :], dst_cols).then_inc(s_dcol, 16)

            def load_part(k, step):
                a, z = PARTS[k]
                src = edge_g[:, ds(step * GPB + a, z - a), :]
                sp.dma_start(ring[:, a:z, :], src).then_inc(s_edge[k], 16)

            def load_rest():
                src = edge_g[:, STEP_GROUPS:STEP_GROUPS + REST, :]
                sp.dma_start(ring[:, 0:REST, :], src).then_inc(s_edge[0], 16)

            def load_x(d):
                sp.wait_ge(s_xc, d)
                sp.dma_start(x_blk[:, :, :], x_g[:, ds(d, 1), :, :].rearrange("p b q f -> p (b q) f")).then_inc(s_x, 16)

            def load_xT(d):
                sp.wait_ge(s_h, 2 * d)
                sp.dma_start(xT[:, :], xt[:, ds(d * NPB, NPB)]).then_inc(s_xT, 16)

            for k in range(len(PARTS)):
                load_part(k, 0)
            sp.dma_start(x_blk[:, :, :], x_g[:, 0, :, :]).then_inc(s_x, 16)
            sp.dma_start(xT[:, :], xt[:, 0:NPB]).then_inc(s_xT, 16)
            sp.dma_start(xT_last[:, :], xt[:, NB * NPB:N]).then_inc(s_xl, 16)
            sp.dma_start(x_last[0:LAST_N, :], x[NB * NPB:N, :]).then_inc(s_xl, 16)

            def next_step(b, x_too, last):
                for k, (a, z) in enumerate(PARTS):
                    sp.wait_ge(s_seg, b * GPB + z)
                    if not last:
                        load_part(k, b + 1)
                    elif k == 0:
                        load_rest()
                    if x_too and k == 2:
                        load_x(b)
                if x_too:
                    load_xT(b)

            fl = on_flag(sp)
            with sp.If(fl == 0):
                next_step(0, False, False)
                with sp.Fori(1, NB - 1) as b:
                    next_step(b, True, False)
                next_step(NB - 1, True, True)
            with sp.Else():
                with sp.Fori(0, NB + 1) as k:
                    with sp.Fori(0, NB) as b:
                        done = k * NB + b
                        for part in range(1, len(PARTS)):
                            sp.wait_ge(s_edge[part], 16 * done + 16)
                        sp.wait_ge(s_edge[0], 16 * done + 16 * k + 16)
                        sp.wait_ge(z_seg, k * NG + b * GPB + 1)
                        for part in range(len(PARTS)):
                            load_part(part, b)
                    sp.wait_ge(z_seg, k * NG + STEP_GROUPS + 1)
                    load_rest()
                with sp.Fori(1, NB) as d:
                    load_x(d)
                    load_xT(d)

            def store(b):
                sp.wait_ge(s_yo, b + 1 + YS)
                sp.dma_start(out_g[:, ds(b, 1), :, :].rearrange("p b q f -> p (b q) f"),
                             xc[:, ds(b * Q, Q), :]).then_inc(s_out, 16)

            with sp.Fori(0, NB) as b:
                store(b)
            sp.wait_ge(s_yo, NB + 1 + YS)
            body = LAST_N - LAST_N % 16
            sp.dma_start(out[NB * NPB:NB * NPB + body, :], xc[0:body, NB * Q, :]).then_inc(s_out, 16)
            sp.dma_start(out[NB * NPB + body:N, :], xc[body:LAST_N, NB * Q, :]).then_inc(s_out, 16)
            sp.wait_ge(s_out, 16 * (NB + 2))

        @block.gpsimd
        def _(pool):
            pool.memset(ident[:, :], 0.0).then_inc(s_const, 1)
            pool.memset(ones[:, :], 1.0).then_inc(s_const, 1)
            pool.memset(eps[:, :], EPS).then_inc(s_const, 1)
            pool.wait_ge(s_const, 1)
            pool.affine_select(out=ident[:, :], in_=ident[:, :], compare_op=ALU.not_equal, fill=1.0, base=0,
                               pattern=[[-1, P]], channel_multiplier=1).then_inc(s_const, 1)
            pool.iota(iota[:, :], pattern=[[1, NPB]], base=0, channel_multiplier=0,
                      allow_small_or_imprecise_dtypes=True).then_inc(s_const, 1)
            pool.memset(vec_rows[:, :], 0.0).then_inc(s_vec0, 1)
            pool.memset(acc[:, :], 0.0).then_inc(s_acc0, 1)
            pool.wait_ge(s_acc0, 1)
            pool.memset(acc_blk[:, :, :], 0.0).then_inc(s_nm, 1)

            def centre(d, src, n, q, n_x):
                pool.wait_ge(s_xm, d + 1)
                if n_x is not None:
                    pool.wait_ge(s_x, n_x)
                else:
                    pool.wait_ge(s_xl, 32)
                mean = x_mean[0:n, 0:q].unsqueeze(2).broadcast_to([n, q, DX])
                pool.tensor_tensor(x_mid[0:n, 0:q, :], src, mean, ALU.subtract).then_inc(s_xmid, 1)
                pool.wait_ge(s_xmid, d + 1)
                pool.tensor_tensor(xc[0:n, ds(d * Q, q), :], x_mid[0:n, 0:q, :],
                                   b2c[0:n, :].unsqueeze(1).broadcast_to([n, q, DX]), ALU.add).then_inc(s_xc, 1)

            def dense(d):
                centre(d, x_blk[:, :, :], P, Q, 16 * d + 16)

            pool.wait_ge(s_b2c, 1)
            with pool.Fori(0, NB) as d:
                dense(d)
            centre(NB, x_last[0:LAST_N, :].unsqueeze(1), LAST_N, 1, None)

            def scale(b, buf, _, n, q):
                pool.wait_ge(s_yrs, b + 1)
                rs = yrs[buf][0:n, 0:q].unsqueeze(2).broadcast_to([n, q, DX])
                pool.tensor_tensor(xc[0:n, ds(b * Q, q), :], y[buf][0:n, 0:q, :], rs, ALU.mult).then_inc(s_yo, 1)

            last_stage(pool, scale)

        @block.scalar
        def _(act):
            act.wait_ge(s_const, 3)
            act.activation(act_spare[:, :], eps[:, :], ACT.Sqrt).then_inc(s_table, 1)
            act.wait_ge(s_dst, 16)
            act.dma_start(w1x[:, :], w1[0:DX, :]).then_inc(s_w, 16)
            act.dma_start(w1e[:, :], w1[DX:DX + F, :]).then_inc(s_w, 16)
            act.dma_start(w1u[:, :], w1[DX + F:DX + F + DU, :]).then_inc(s_w, 16)
            act.dma_start(w2s[:, :, :], w2.rearrange("(j p) n -> p j n", j=2)).then_inc(s_w, 16)
            act.wait_ge(s_vec0, 1)
            act.dma_start(vec_rows[6:7, 0:DU], u[0:1, :]).then_inc(s_w, 16)
            for k, vec in enumerate((b1, gamma, beta)):
                act.dma_start(vec_rows[2 * k:2 * k + 2, :], vec.rearrange("(j p) -> j p", j=2)).then_inc(s_w, 16)
            act.dma_start(b2s[:, :], b2.unsqueeze(0).broadcast_to([P, DX])).then_inc(s_w, 16)
            fl = on_flag(act)

            def mean_x(d, src, n, q, n_x):
                if n_x is not None:
                    act.wait_ge(s_x, n_x)
                else:
                    act.wait_ge(s_xl, 32)
                    act.wait_ge(s_xc, NB)
                for k in range(q):
                    last = act.activation(x_junk[0:n, k, :], src[:, k, :], ACT.Identity, scale=1.0 / DX,
                                          accum_out=x_mean[0:n, k:k + 1])
                last.then_inc(s_xm, 1)

            def dense(d, last=False, fast=False):
                n, q = (LAST_N, 1) if last else (P, Q)
                w = n * q
                if last:
                    mean_x(d, x_last[0:n, :].unsqueeze(1), n, q, None)
                else:
                    mean_x(d, x_blk[:, :, :], n, q, 16 * d + 16)
                act.wait_ge(s_nm, d + 1)
                if fast:
                    act.wait_ge(s_acc, (d + 1) * GPB + MARGIN + GPB)
                act.activation(acc_blk[:, 0:q, 0:n], acc[:, ds(d * NPB, w)].rearrange("r (p q) -> r q p", q=q),
                               ACT.Identity).then_inc(s_blk, 1)
                act.wait_ge(s_mT, d + 2)
                act.activation(meanT[:, 0:w], ps_ft[0:F, 0:w], ACT.Identity).then_inc(s_mTs, 1)
                for j in range(2):
                    act.wait_ge(s_h, 2 * d + j + 1)
                    act.activation(hT[:, j, ds(d * NPB, w)], ps_h[j][:, 0:w], ACT.Identity,
                                   bias=hb[:, j:j + 1]).then_inc(s_hs, 1)

            act.wait_ge(s_hbs, 1)
            with act.If(fl == 0):
                with act.Fori(0, NB - 1) as d:
                    dense(d, fast=True)
            with act.Else():
                act.wait_ge(z_fill, 1)
                with act.Fori(0, NB - 1) as d:
                    dense(d)
            act.wait_ge(s_final, 1)
            dense(NB - 1)
            dense(NB, last=True)

            act.wait_ge(s_mv, 2)
            act.activation(sd[:, :], mv[:, :, 1], ACT.Sqrt, bias=eps[:, 0:1]).then_inc(s_sd, 1)

            def relu_and_root(b, buf, rbuf, n, q):
                act.wait_ge(s_y, b + 1)
                for j in range(2):
                    act.activation(rT[rbuf][:, j, 0:n * q], hT[:, j, ds(b * NPB, n * q)], ACT.Relu,
                                   bias=bn_t[:, j:j + 1], scale=bn_s[:, j:j + 1]).then_inc(s_r, 1)
                lagging(b, buf, root)

            def root(b, buf, n, q):
                act.wait_ge(s_sq, b + 1)
                act.activation(ysd[buf][0:n, 0:q], ssq[buf][0:n, 0:q], ACT.Sqrt, bias=eps[0:n, 0:1],
                               scale=1.0 / DX).then_inc(s_ysd, 1)

            act.wait_ge(s_bn, 4)
            last_stage(act, relu_and_root)
            flush(root)

        @block.tensor
        def _(pe):
            def warm_up(n):
                for _ in range(n):
                    pe.matmul(ps_h[0][:, :], warm[:, 0:P], warm[:, :], start=True, stop=True)

            pe.wait_ge(s_warm, 1)
            warm_up(12)
            pe.wait_ge(s_const, 4)
            pe.wait_ge(s_base, 1)
            for t in range(2):
                ins = pe.matmul(seg[2][:, t:NG:2], base[:, t:t + 1].broadcast_to([PAIRS, P]),
                                ident[0:PAIRS, 0:PAIRS], start=True, stop=True)
            ins.then_inc(s_rows, 1)
            pe.wait_ge(s_bad, 1)
            pe.matmul(seg[3][0:1, 0:2], ones[0:PAIRS, :], bad[:, 2, :], start=True, stop=True).then_inc(s_nbad, 1)
            warm_up(8)
            fl = on_flag(pe)

            def transpose_vectors():
                pe.wait_ge(s_w, 16 * 9)
                pe.transpose(ps_nm[:, 0:7], vec_rows[:, :], ident[0:7, 0:7]).then_inc(s_vecT, 1)

            def hidden_of_u():
                pe.wait_ge(s_vecs, 1)
                for j in range(2):
                    ins = pe.matmul(ps_nm[:, 8 + j:9 + j], w1u[:, j * P:(j + 1) * P], vecs[0:DU, 6:7],
                                    start=True, stop=True)
                ins.then_inc(s_hb, 1)

            def sum_group(ps, rows, onehots, done):
                for s in range(SLOTS):
                    ins = pe.matmul(ps, rows[s], onehots[s], start=s == 0, stop=s == SLOTS - 1)
                ins.then_inc(done, 1)

            def to_nodes(d, last=False):
                n, q = (LAST_N, 1) if last else (P, Q)
                pe.wait_ge(s_blk, d + 1)
                for k in range(q):
                    ins = pe.transpose(ps_nm[0:n, k * P:k * P + R], acc_blk[:, k, 0:n], ident[0:R, 0:R])
                ins.then_inc(s_nm, 1)

            def to_features(d, last=False):
                n, q = (LAST_N, 1) if last else (P, Q)
                pe.wait_ge(s_mTs, d + 1)
                pe.wait_ge(s_mean, d + 1)
                for k in range(q):
                    ins = pe.transpose(ps_ft[0:F, k * n:(k + 1) * n], mean_nm[0:n, k, :], ident[0:n, 0:n])
                ins.then_inc(s_mT, 1)

            def hidden_x(d, j, w=NPB):
                if w == NPB:
                    pe.wait_ge(s_xT, 16 * d + 16)
                else:
                    pe.wait_ge(s_xl, 32)
                pe.wait_ge(s_hs, 2 * d + j + 1)
                pe.matmul(ps_h[j][:, 0:w], w1x[:, j * P:(j + 1) * P], (xT if w == NPB else xT_last)[:, 0:w],
                          start=True, stop=False)

            def hidden_e(d, j, w=NPB):
                pe.wait_ge(s_mTs, d + 2)
                pe.matmul(ps_h[j][:, 0:w], w1e[:, j * P:(j + 1) * P], meanT[:, 0:w], start=False,
                          stop=True).then_inc(s_h, 1)

            def group(b, j):
                pe.wait_ge(s_oh, b * GPB + j + 1)
                pe.wait_ge(s_acc, b * GPB + earlier_user(j) + 1 + GPB)
                sum_group(seg[bank_of(j)][0:R, 0:W], ring_s[j], [onehot[:, j, s, :] for s in range(SLOTS)], s_seg)

            def step(b, dense):
                starts = {a: k for k, (a, _) in enumerate(PARTS)}
                for j in range(GPB):
                    if j in starts:
                        pe.wait_ge(s_edge[starts[j]], 16 * b + 16)
                    group(b, j)
                    if not dense:
                        if j == 12:
                            transpose_vectors()
                        if j == 15:
                            hidden_of_u()
                        continue
                    if j == MARGIN + 3:
                        to_nodes(b - 1)
                    if j == MARGIN + 6:
                        to_features(b - 1)
                    for k in range(2):
                        if j == MARGIN + 8 + 2 * k:
                            hidden_x(b - 1, k)
                            hidden_e(b - 1, k)

            with pe.If(fl == 0):
                step(0, False)
                with pe.Fori(1, NB) as b:
                    step(b, True)
                pe.wait_ge(s_edge[0], 16 * NB + 16)
                for j in range(REST):
                    group(NB, j)
            with pe.Else():
                transpose_vectors()
                hidden_of_u()

                def slow_group(n, rows):
                    pe.wait_ge(z_oh, n + 1)
                    sum_group(seg[3][0:R, :], rows, [wide[:, s * NPB:(s + 1) * NPB] for s in range(SLOTS)], z_seg)

                with pe.Fori(0, NB + 1) as k:
                    with pe.Fori(0, NB) as b:
                        for part in range(1, len(PARTS)):
                            pe.wait_ge(s_edge[part], 16 * (k * NB + b) + 32)
                        pe.wait_ge(s_edge[0], 16 * (k * NB + b) + 16 * k + 32)
                        for j in range(GPB):
                            slow_group(k * NG + b * GPB + j, ring_s[j])
                    pe.wait_ge(s_edge[0], 16 * (k * NB + NB) + 16 * k + 32)
                    for j in range(REST):
                        slow_group(k * NG + STEP_GROUPS + j, ring_s[j])
                with pe.Fori(0, NB - 1) as d:
                    to_nodes(d)
                    to_features(d)
                    for j in range(2):
                        hidden_x(d, j)
                        hidden_e(d, j)
            d = NB - 1
            for j in range(2):
                hidden_x(d, j)
            to_nodes(d)
            to_features(d)
            for j in range(2):
                hidden_e(d, j)
            to_nodes(NB, last=True)
            to_features(NB, last=True)
            for j in range(2):
                hidden_x(NB, j, LAST_N)
                hidden_e(NB, j, LAST_N)

            def second(b, buf, rbuf, n, q):
                pe.wait_ge(s_r, 2 * b + 2)
                pe.wait_ge(s_ys, b + 1)
                for k in range(q):
                    for j in range(2):
                        ins = pe.matmul(seg[buf][0:n, k * DX:(k + 1) * DX], rT[rbuf][:, j, k * n:(k + 1) * n],
                                        w2c[:, j, :], start=j == 0, stop=j == 1)
                ins.then_inc(s_y, 1)

            pe.wait_ge(s_w2, 2)
            last_stage(pe, second)

        @block.vector
        def _(dve):
            pro = [0]

            def own(ins):
                pro[0] += 1
                ins.then_inc(s_pro, 1)
                dve.wait_ge(s_pro, pro[0])

            dve.memset(warm[:, :], 1.0).then_inc(s_warm, 1)
            dve.memset(spare[:, 7:8], 0.0).then_inc(s_mT, 1)
            dve.memset(spare[:, 8:9], 0.0).then_inc(s_mTs, 1)
            dve.memset(spare[:, 9:10], 0.0).then_inc(s_hs, 2)
            dve.wait_ge(s_dst, 16)
            dve.tensor_reduce(base[:, :], D[:, :, :].bitcast(mybir.dt.uint32), AX.X, ALU.min).then_inc(s_base, 1)
            own(dve.tensor_reduce(most[:, :], D[:, :, :], AX.X, ALU.max))
            dve.wait_ge(s_base, 1)
            dve.wait_ge(s_low, 16)
            dve.tensor_tensor(bad[:, 0, :], base[:, :], low[:, :], ALU.is_lt)
            own(dve.tensor_tensor(span[:, :], most[:, :], base[:, :], ALU.subtract))
            own(dve.tensor_scalar(bad[:, 1, :], span[:, :], float(W), None, ALU.is_ge))
            own(dve.scalar_tensor_tensor(bad[:, 1, :], base[:, :], float(N), bad[:, 1, :], ALU.is_ge, ALU.add))
            dve.tensor_tensor(bad[:, 2, :], bad[:, 0, :], bad[:, 1, :], ALU.add).then_inc(s_bad, 1)
            dve.wait_ge(s_rows, 1)
            dve.tensor_scalar(base_row[0:1, 0:NB, 0:GPB],
                              seg[2][0:1, 0:STEP_GROUPS].rearrange("o (b g) -> o b g", g=GPB),
                              0.0, float(N - 1), ALU.max, ALU.min).then_inc(s_brow, 1)
            dve.tensor_scalar(base_row[0:1, NB, 0:REST], seg[2][0:1, STEP_GROUPS:NG],
                              0.0, float(N - 1), ALU.max, ALU.min).then_inc(s_brow, 1)
            dve.wait_ge(s_dcol, 16)
            dve.tensor_tensor(dloc[:, :, :], dcols[:, :, :],
                              seg[2][:, 0:NG].unsqueeze(2).broadcast_to([P, NG, SLOTS]),
                              ALU.subtract).then_inc(s_dloc, 1)
            dve.wait_ge(s_nbad, 1)
            own(dve.tensor_reduce(x_mean[0:1, 0:1], seg[3][0:1, 0:2], AX.X, ALU.add))
            dve.tensor_scalar(flag[0:1, 0:1], x_mean[0:1, 0:1], 0.5, None, ALU.is_ge).then_inc(s_flag, 1)
            dve.wait_ge(s_brow, 2)
            dve.wait_ge(s_dloc, 1)
            dve.wait_ge(s_acc0, 1)
            fl = on_flag(dve)

            def take_vectors():
                dve.wait_ge(s_vecT, 1)
                dve.tensor_copy(vecs[:, :], ps_nm[:, 0:7]).then_inc(s_vecs, 1)

            def hidden_constant():
                dve.wait_ge(s_vecs, 1)
                dve.wait_ge(s_hb, 1)
                dve.tensor_tensor(hb[:, :], ps_nm[:, 8:10], vecs[:, 0:2], ALU.add).then_inc(s_hbs, 1)

            def centre_weights():
                dve.wait_ge(s_w, 16 * 9)
                dve.tensor_reduce(b2m[:, :], b2s[:, :], AX.X, ALU.add).then_inc(s_small, 1)
                dve.tensor_reduce(w2m[:, :], w2s[:, :, :], AX.X, ALU.add).then_inc(s_small, 1)
                dve.wait_ge(s_small, 2)
                dve.tensor_scalar(b2m[:, :], b2m[:, :], 1.0 / DX, None, ALU.mult).then_inc(s_small, 1)
                dve.tensor_scalar(w2m[:, :], w2m[:, :], 1.0 / DX, None, ALU.mult).then_inc(s_small, 1)
                dve.wait_ge(s_small, 4)
                dve.tensor_scalar(b2c[:, :], b2s[:, :], b2m[:, 0:1], None, ALU.subtract).then_inc(s_b2c, 1)
                for j in range(2):
                    dve.tensor_scalar(w2c[:, j, :], w2s[:, j, :], w2m[:, j:j + 1], None,
                                      ALU.subtract).then_inc(s_w2, 1)

            def inverse(d, last=False):
                n, q = (LAST_N, 1) if last else (P, Q)
                dve.wait_ge(s_nm, d + 2)
                counts = ps_nm[0:n, :].rearrange("p (q f) -> p q f", f=P)[:, 0:q, CNT]
                dve.tensor_scalar(cnt1[0:n, 0:q], counts, 1.0, None, ALU.max).then_inc(s_cnt, 1)
                dve.wait_ge(s_cnt, d + 1)
                dve.reciprocal(inv[0:n, 0:q], cnt1[0:n, 0:q]).then_inc(s_inv, 1)

            def means(d, last=False):
                n, q = (LAST_N, 1) if last else (P, Q)
                dve.wait_ge(s_inv, d + 1)
                dve.wait_ge(s_mT, d + 1)
                sums = ps_nm[0:n, :].rearrange("p (q f) -> p q f", f=P)[:, 0:q, 0:F]
                dve.tensor_tensor(mean_nm[0:n, 0:q, :], sums, inv[0:n, 0:q].unsqueeze(2).broadcast_to([n, q, F]),
                                  ALU.mult).then_inc(s_mean, 1)

            def statistics(d, w=NPB):
                for j in range(2):
                    dve.wait_ge(s_hs, 2 * d + j + 3)
                    dve.bn_stats(stats[:, j, ds(d, 1), :].rearrange("p b k -> p (b k)"),
                                 hT[:, j, ds(d * NPB, w)]).then_inc(s_st, 1)

            def one_hot(b, j):
                group = b * GPB + j
                where = dloc[:, ds(group, 1), :].rearrange("p g s -> p (g s)").unsqueeze(2).broadcast_to([P, SLOTS, W])
                nodes = iota[:, 0:W].unsqueeze(1).broadcast_to([P, SLOTS, W])
                dve.tensor_tensor(onehot[:, j % GPB, :, :], nodes, where, ALU.is_equal).then_inc(s_oh, 1)

            def bases(b, n):
                row = base_row[0:1, ds(b, 1), 0:n].rearrange("o b g -> o (b g)")
                _, vals = nc.values_load_multi_w_load_instructions(
                    row, engines=[mybir.EngineType.DVE], min_val=0, max_val=N - 1,
                    skip_runtime_bounds_check_because="base_row is clamped to these bounds when it is written")
                return vals

            def add_group(b, j, at, final=False):
                dve.wait_ge(s_seg, b * GPB + j + 1)
                dve.wait_ge(s_acc, b * GPB + j + GPB)
                window = acc[:, ds(at, W)]
                ins = dve.tensor_tensor(window, window, seg[bank_of(j)][0:R, 0:W], ALU.add)
                ins.then_inc(s_final if final else s_acc, 1)

            def step(b, dense):
                at = bases(b, GPB)
                for j in range(GPB):
                    one_hot(b, j + LEAD)
                    add_group(b, j, at[j])
                    if not dense:
                        if j == 13:
                            take_vectors()
                        continue
                    if j == MARGIN + 3:
                        inverse(b - 1)
                    if j == MARGIN + 4:
                        means(b - 1)
                if dense:
                    statistics(b - 1)

            with dve.If(fl == 0):
                dve.memset(spare[:, 0:1], 0.0).then_inc(s_acc, GPB)
                for j in range(LEAD):
                    one_hot(0, j)
                step(0, False)
                hidden_constant()
                centre_weights()
                with dve.Fori(1, NB) as b:
                    step(b, True)
                at = bases(NB, REST)
                for j in range(REST):
                    add_group(NB, j, at[j], final=j == REST - 1)
            with dve.Else():
                dve.tensor_copy(dloc[:, :, :], dcols[:, :, :]).then_inc(s_dloc, 1)
                take_vectors()
                hidden_constant()
                centre_weights()
                dve.wait_ge(s_dloc, 2)
                flat = dloc[:, :, :].rearrange("p g s -> p (g s)")

                def slow_group(k, g):
                    n = k * NG + g
                    for s in range(SLOTS):
                        ins = dve.tensor_scalar(wide[:, s * NPB:(s + 1) * NPB], iota[:, :],
                                                flat[:, ds(g * SLOTS + s, 1)], None, ALU.is_equal)
                    ins.then_inc(z_oh, 1)
                    dve.wait_ge(z_seg, n + 2)
                    cols = acc[:, ds(k * NPB, NPB)]
                    dve.tensor_tensor(cols, cols, seg[3][0:R, :], ALU.add).then_inc(z_acc, 1)
                    dve.wait_ge(z_acc, n + 1)

                dve.memset(spare[:, 1:2], 0.0).then_inc(z_seg, 1)
                with dve.Fori(0, NB + 1) as k:
                    with dve.Fori(0, NG) as g:
                        slow_group(k, g)
                    dve.tensor_scalar(flat, flat, float(NPB), None, ALU.subtract).then_inc(z_sh, 1)
                    dve.wait_ge(z_sh, k + 1)
                dve.memset(spare[:, 2:3], 0.0).then_inc(z_fill, 1)
                with dve.Fori(0, NB - 1) as d:
                    inverse(d)
                    means(d)
                    statistics(d)
                dve.memset(spare[:, 3:4], 0.0).then_inc(s_final, 1)
            inverse(NB - 1)
            means(NB - 1)
            statistics(NB - 1)
            inverse(NB, last=True)
            means(NB, last=True)
            statistics(NB, LAST_N)

            dve.wait_ge(s_st, 2 * (NB + 1))
            for j in range(2):
                dve.bn_aggr(mv[:, j, :], stats[:, j, :, :].rearrange("p b k -> p (b k)")).then_inc(s_mv, 1)
            dve.wait_ge(s_mv, 2)
            dve.wait_ge(s_sd, 1)
            dve.reciprocal(rsd[:, :], sd[:, :]).then_inc(s_bn, 1)
            dve.wait_ge(s_bn, 1)
            dve.tensor_tensor(bn_s[:, :], rsd[:, :], vecs[:, 2:4], ALU.mult).then_inc(s_bn, 1)
            dve.wait_ge(s_bn, 2)
            dve.tensor_tensor(bn_ms[:, :], mv[:, :, 0], bn_s[:, :], ALU.mult).then_inc(s_bn, 1)
            dve.wait_ge(s_bn, 3)
            dve.tensor_tensor(bn_t[:, :], vecs[:, 4:6], bn_ms[:, :], ALU.subtract).then_inc(s_bn, 1)
            dve.memset(spare[:, 4:5], 0.0).then_inc(s_y, 2)
            dve.memset(spare[:, 5:6], 0.0).then_inc(s_ys, YS)
            dve.memset(spare[:, 6:7], 0.0).then_inc(s_yo, YS)

            def finish(b, buf, _, n, q):
                dve.wait_ge(s_y, b + 3)
                dve.wait_ge(s_yo, b + 1)
                dve.tensor_tensor(y[buf][0:n, 0:q, :], seg[buf][0:n, 0:q * DX].rearrange("p (q f) -> p q f", q=q),
                                  xc[0:n, ds(b * Q, q), :], ALU.add).then_inc(s_ys, 1)
                dve.wait_ge(s_ys, b + 1 + YS)
                for k in range(q):
                    ins = dve.tensor_tensor_reduce(
                        out=y_sq[buf][0:n, k, :], in0=y[buf][0:n, k, :], in1=y[buf][0:n, k, :], scale=1.0,
                        scalar=0.0, op0=ALU.mult, op1=ALU.add, accum_out=ssq[buf][0:n, k:k + 1])
                ins.then_inc(s_sq, 1)
                lagging(b, buf, inverse_sd)

            def inverse_sd(b, buf, n, q):
                dve.wait_ge(s_ysd, b + 1)
                dve.reciprocal(yrs[buf][0:n, 0:q], ysd[buf][0:n, 0:q]).then_inc(s_yrs, 1)

            dve.wait_ge(s_xc, NB + 1)
            last_stage(dve, finish)
            flush(inverse_sd)


def kernel(x, src, dst, edge_attr_96, L0_gnn_u, L0_gnn_W1, L0_gnn_b1, L0_gnn_gamma, L0_gnn_beta, L0_gnn_W2,
           L0_gnn_b2):
    import concourse.bacc as _bacc
    from concourse import mybir as _mybir
    from concourse.bass_utils import run_bass_kernel_spmd as _run

    edge, dst = np.asarray(edge_attr_96), np.asarray(dst)
    edge = np.pad(np.pad(edge, ((0, NG * GE - E), (0, 0))), ((0, 0), (0, 1)), constant_values=1)
    dst = np.pad(dst, (0, NG * GE - E), constant_values=-1)
    x = np.asarray(x)
    blocks = x[:NB * NPB].reshape(NB, P, Q, DX).transpose(3, 0, 2, 1).reshape(DX, NB * NPB)
    xt = np.concatenate([blocks, x[NB * NPB:].T], axis=1)

    nc = _bacc.Bacc("TRN2", target_bir_lowering=False, num_devices=1)
    arrays, args = {}, []
    for name, a in (("x", x), ("xt", xt), ("dst_rows", dst.reshape(PAIRS, 2, GE)),
                    ("dst_cols", dst.reshape(NG, P, SLOTS).transpose(1, 0, 2)), ("edge", edge),
                    ("u", L0_gnn_u), ("w1", L0_gnn_W1), ("b1", L0_gnn_b1), ("gamma", L0_gnn_gamma),
                    ("beta", L0_gnn_beta), ("w2", L0_gnn_W2), ("b2", L0_gnn_b2), ("lowest", lower_bounds())):
        a = np.ascontiguousarray(a)
        arrays[f"in_{name}"] = a
        args.append(nc.dram_tensor(f"in_{name}", a.shape, _mybir.dt.from_np(a.dtype), kind="ExternalInput").ap())
    args.append(nc.dram_tensor("out_0", (N, DX), _mybir.dt.float32, kind="ExternalOutput").ap())
    gnn_kernel(nc, *args)
    r = _run(nc, [arrays], core_ids=[0])
    return r.results[0]["out_0"]
```

```python
import numpy as np
import concourse.bass as bass
from concourse import mybir
from contextlib import ExitStack

N, DX, F, DU, HID = 6250, 128, 96, 64, 256
E = 106250
EPS = 1e-5
P = 128

SLOTS = 4
GE = P * SLOTS
NG = -(-E // GE)
W = 56
NPB = 512
Q = NPB // P
NB = N // NPB
LAST_N = N - NB * NPB
GPB = 17
STEP_GROUPS = NB * GPB
REST = NG - STEP_GROUPS
MARGIN = 5
PARTS = [(0, 5), (5, 9), (9, 13), (13, 17)]
AT_INVERSE, AT_MEANS, AT_HIDDEN, AT_STATISTICS = (8, 9, 10), 11, (13, 14), (15, 16)
T = 32
YS = 4
LAG_INV, LAG_ROOT = 2, 3
LEAD = 4
EARLY = 2
R = F + 1
CNT = F
ACC_W = (NB + 1) * NPB
PAIRS = NG // 2
assert GPB * GE * NB * P <= E * P and E * NPB // N // GE == GPB
assert MARGIN <= AT_INVERSE[0] and AT_INVERSE[-1] < AT_MEANS < AT_HIDDEN[0] and AT_HIDDEN[-1] < AT_STATISTICS[0]
assert NG == 2 * PAIRS and 0 < REST <= min(PARTS[0][1], LEAD) and ACC_W >= N + W


def bank_of(j):
    return j % 4 if j < 8 else (j - 8) % 3


def earlier_user(j):
    i = j - 1
    while bank_of(i % GPB) != bank_of(j):
        i -= 1
    return i


def last_stage(eng, do, blocks=NB + 1):
    peeled = LAG_ROOT
    for b in range(peeled):
        do(b, b % YS, P, Q)
    turns = (NB - peeled) // YS
    with eng.Fori(0, turns) as i:
        for k in range(peeled, peeled + YS):
            do(i * YS + k, k % YS, P, Q)
    for b in range(peeled + turns * YS, min(blocks, NB)):
        do(b, b % YS, P, Q)
    if blocks > NB:
        do(NB, NB % YS, LAST_N, 1)


def lagging(b, buf, lag, do):
    if not isinstance(b, int) or b >= lag:
        do(b - lag, (buf - lag) % YS, P, Q)


def flush(lag, do):
    for b in range(NB + 1 - lag, NB):
        do(b, b % YS, P, Q)
    do(NB, NB % YS, LAST_N, 1)


def lower_bounds():
    g = np.arange(NG)
    return np.where(g >= MARGIN, NPB * ((g - MARGIN) // GPB), 0).reshape(PAIRS, 2).astype(np.float32)


def gnn_kernel(nc, x, xt, dst_rows, dst_cols, edge, u, w1, b1, gamma, beta, w2, b2, lowest, out):
    fp32, bf16, i32 = mybir.dt.float32, mybir.dt.bfloat16, mybir.dt.int32
    ALU, ACT, AX = mybir.AluOpType, mybir.ActivationFunctionType, mybir.AxisListType
    ds = bass.ds

    with ExitStack() as ctx:
        def sb(name, shape, dt=fp32):
            return ctx.enter_context(nc.sbuf_tensor(name, shape, dt))

        def sem(name):
            return ctx.enter_context(nc.semaphore(name))

        ring = sb("ring", [P, GPB, SLOTS * R])
        onehot = sb("onehot", [P, GPB, SLOTS, W])
        acc = sb("acc", [R, ACC_W])
        mean_nm = sb("mean_nm", [P, Q, F])
        meanT = sb("meanT", [F, NPB])
        cnt_rows = sb("cnt_rows", [F, NPB])
        cntT = sb("cntT", [F, NPB // T, T])
        cntT_1 = sb("cntT_1", [F, NPB // T])
        cntT_inv = sb("cntT_inv", [F, NPB // T])
        inv_rows = sb("inv_rows", [F, NPB])
        x_blk = sb("x_blk", [P, Q, DX])
        x_last = sb("x_last", [P, DX])
        xT = sb("xT", [DX, NPB])
        xT_end = sb("xT_end", [DX, NPB + LAST_N])
        xc = sb("xc", [P, (NB + 1) * Q, DX])
        x_mid = sb("x_mid", [P, Q, DX])
        x_junk = sb("x_junk", [P, Q + 1, DX])
        x_mean = sb("x_mean", [P, Q])
        x_mean_last = sb("x_mean_last", [P, 1])
        meanT_last = sb("meanT_last", [F, LAST_N])
        mean_last = sb("mean_last", [P, F])
        cnt1 = sb("cnt1", [P, Q + 1])
        inv = sb("inv", [P, Q + 1])
        hT = sb("hT", [P, 2, N])
        stats = sb("stats", [P, 2, NB + 1, 6])
        D = sb("D", [PAIRS, 2, GE], i32)
        dcols = sb("dcols", [P, NG, SLOTS], i32)
        dloc = sb("dloc", [P, NG, SLOTS])
        base = sb("base", [PAIRS, 2])
        most = sb("most", [PAIRS, 2])
        span = sb("span", [PAIRS, 2])
        low = sb("low", [PAIRS, 2])
        bad = sb("bad", [PAIRS, 3, 2])
        base_row = sb("base_row", [1, NB + 1, 20], i32)
        flag = sb("flag", [1, 1], i32)
        iota = sb("iota", [P, NPB])
        ident = sb("ident", [P, P])
        ones = sb("ones", [P, 1])
        eps = sb("eps", [P, 1])
        w1x = sb("w1x", [DX, HID])
        w1e = sb("w1e", [F, HID])
        w1u = sb("w1u", [DU, HID])
        w2s = sb("w2s", [P, 2, DX])
        w2c = sb("w2c", [P, 2, DX])
        w2m = sb("w2m", [P, 2])
        vec_rows = sb("vec_rows", [7, P])
        vecs = sb("vecs", [P, 7])
        hb = sb("hb", [P, 2])
        b2s = sb("b2s", [P, DX])
        b2c = sb("b2c", [P, DX])
        b2m = sb("b2m", [P, 1])
        mv = sb("mv", [P, 2, 2])
        sd = sb("sd", [P, 2])
        rsd = sb("rsd", [P, 2])
        bn_s = sb("bn_s", [P, 2])
        bn_t = sb("bn_t", [P, 2])
        bn_nm = sb("bn_nm", [P, 2])
        bn_h = sb("bn_h", [P, NPB])
        y = [sb(f"y{k}", [P, Q, DX]) for k in range(YS)]
        ssq = [sb(f"ssq{k}", [P, Q]) for k in range(YS)]
        ysd = [sb(f"ysd{k}", [P, Q]) for k in range(YS)]
        yrs = [sb(f"yrs{k}", [P, Q]) for k in range(YS)]
        warm = sb("warm", [P, NPB], bf16)
        spare = sb("spare", [P, 10])
        act_spare = sb("act_spare", [P, 1])

        seg = [ctx.enter_context(nc.psum_tensor(f"seg{k}", [P, 512], fp32)) for k in range(4)]
        ps_ft = ctx.enter_context(nc.psum_tensor("ps_ft", [P, 512], fp32))
        ps_nm = ctx.enter_context(nc.psum_tensor("ps_nm", [P, 512], fp32))
        ps_h = [ctx.enter_context(nc.psum_tensor(f"ps_h{j}", [P, 512], fp32)) for j in range(2)]

        s_dst = sem("s_dst")
        s_dcol = sem("s_dcol")
        s_dcol_rest = sem("s_dcol_rest")
        s_low = sem("s_low")
        s_w = sem("s_w")
        s_vec = sem("s_vec")
        s_edge = [sem(f"s_edge{k}") for k in range(len(PARTS))]
        s_x = sem("s_x")
        s_xl = sem("s_xl")
        s_const = sem("s_const")
        s_iota = sem("s_iota")
        s_vec0 = sem("s_vec0")
        s_warm = sem("s_warm")
        s_table = sem("s_table")
        s_acc0 = sem("s_acc0")
        s_pro = sem("s_pro")
        s_dloc = sem("s_dloc")
        s_base = sem("s_base")
        s_rows = sem("s_rows")
        s_brow = sem("s_brow")
        s_most = sem("s_most")
        s_bad = sem("s_bad")
        s_nbad = sem("s_nbad")
        s_flag = sem("s_flag")
        s_vecT = sem("s_vecT")
        s_vecs = sem("s_vecs")
        s_small = sem("s_small")
        s_hb = sem("s_hb")
        s_hbs = sem("s_hbs")
        s_w2 = sem("s_w2")
        s_b2c = sem("s_b2c")
        s_oh = sem("s_oh")
        s_seg = sem("s_seg")
        s_acc = sem("s_acc")
        s_final = sem("s_final")
        s_cnt0 = sem("s_cnt0")
        s_rowsc = sem("s_rowsc")
        s_cntT = sem("s_cntT")
        s_cnt1 = sem("s_cnt1")
        s_invT = sem("s_invT")
        s_inv_rows = sem("s_inv_rows")
        s_nm = sem("s_nm")
        s_cnt = sem("s_cnt")
        s_inv = sem("s_inv")
        s_mean = sem("s_mean")
        s_mT = sem("s_mT")
        s_mTs = sem("s_mTs")
        s_mTl = sem("s_mTl")
        s_mTls = sem("s_mTls")
        s_xT = sem("s_xT")
        s_xm = sem("s_xm")
        s_xmid = sem("s_xmid")
        s_xc = sem("s_xc")
        s_h = sem("s_h")
        s_hs = sem("s_hs")
        s_st = sem("s_st")
        s_mv = sem("s_mv")
        s_sd = sem("s_sd")
        s_bn = sem("s_bn")
        s_r = sem("s_r")
        s_r0 = sem("s_r0")
        s_y = sem("s_y")
        s_ys = sem("s_ys")
        s_sq = sem("s_sq")
        s_ysd = sem("s_ysd")
        s_yrs = sem("s_yrs")
        s_yo = sem("s_yo")
        s_yo_full = sem("s_yo_full")
        s_yo_last = sem("s_yo_last")
        s_out = sem("s_out")
        s_out_last = sem("s_out_last")
        z_oh = sem("z_oh")
        z_seg = sem("z_seg")
        z_acc = sem("z_acc")
        z_sh = sem("z_sh")
        z_fill = sem("z_fill")

        ring_s = [[ring[:, j, s * R:(s + 1) * R] for s in range(SLOTS)] for j in range(GPB)]
        free = ring[:, :, :].rearrange("p g e -> p (g e)")
        rT = [free[:, k * 2 * NPB:(k + 1) * 2 * NPB].rearrange("p (j n) -> p j n", j=2) for k in range(YS)]
        free = free[:, YS * 2 * NPB:]
        y_sq = [free[:, k * NPB:(k + 1) * NPB].rearrange("p (q f) -> p q f", q=Q) for k in range(YS)]
        wide = onehot[:, :, :, :].rearrange("p g s w -> p (g s w)")[:, 0:SLOTS * NPB]

        edge_g = edge.rearrange("(g p s) f -> p g (s f)", p=P, s=SLOTS)
        x_g = x[0:NB * NPB, :].rearrange("(b p q) f -> p b q f", p=P, q=Q)
        out_g = out[0:NB * NPB, :].rearrange("(b p q) f -> p b q f", p=P, q=Q)

        block = ctx.enter_context(nc.Block())

        def on_flag(eng):
            eng.wait_ge(s_flag, 1)
            return eng.value_load(flag[0:1, 0:1], min_val=0, max_val=1)

        @block.sync
        def _(sp):
            sp.dma_start(D[:, :, :], dst_rows).then_inc(s_dst, 16)
            sp.dma_start(low[:, :], lowest).then_inc(s_low, 16)
            soon = GPB + LEAD
            sp.dma_start(dcols[:, 0:soon, :], dst_cols[:, 0:soon, :]).then_inc(s_dcol, 16)

            def load_part(k, step):
                a, z = PARTS[k]
                src = edge_g[:, ds(step * GPB + a, z - a), :]
                sp.dma_start(ring[:, a:z, :], src).then_inc(s_edge[k], 16)

            def load_rest():
                src = edge_g[:, STEP_GROUPS:STEP_GROUPS + REST, :]
                sp.dma_start(ring[:, 0:REST, :], src).then_inc(s_edge[0], 16)

            def load_x(d):
                sp.wait_ge(s_xc, d)
                sp.dma_start(x_blk[:, :, :], x_g[:, ds(d, 1), :, :].rearrange("p b q f -> p (b q) f")).then_inc(s_x, 16)

            def load_xT(d):
                sp.wait_ge(s_h, 2 * d)
                sp.dma_start(xT[:, :], xt[:, ds(d * NPB, NPB)]).then_inc(s_xT, 16)

            load_part(0, 0)
            sp.dma_start(dcols[:, soon:NG, :], dst_cols[:, soon:NG, :]).then_inc(s_dcol_rest, 16)
            for k in range(1, len(PARTS)):
                load_part(k, 0)
            sp.dma_start(x_blk[:, :, :], x_g[:, 0, :, :]).then_inc(s_x, 16)
            sp.dma_start(xT[:, :], xt[:, 0:NPB]).then_inc(s_xT, 16)

            def load_last_x():
                sp.dma_start(xT_end[:, :], xt[:, (NB - 1) * NPB:N]).then_inc(s_xl, 16)
                sp.dma_start(x_last[0:LAST_N, :], x[NB * NPB:N, :]).then_inc(s_xl, 16)

            def next_step(b, x_too, last):
                for k, (a, z) in enumerate(PARTS):
                    sp.wait_ge(s_seg, b * GPB + z)
                    if not last:
                        load_part(k, b + 1)
                    elif k == 0:
                        load_rest()
                    if x_too and k == 2:
                        load_x(b)
                if x_too and not last:
                    load_xT(b)

            fl = on_flag(sp)
            with sp.If(fl == 0):
                next_step(0, False, False)
                load_last_x()
                with sp.Fori(1, NB - 1) as b:
                    next_step(b, True, False)
                next_step(NB - 1, True, True)
            with sp.Else():
                load_last_x()
                with sp.Fori(0, NB + 1) as k:
                    with sp.Fori(0, NB) as b:
                        done = k * NB + b
                        for part in range(1, len(PARTS)):
                            sp.wait_ge(s_edge[part], 16 * done + 16)
                        sp.wait_ge(s_edge[0], 16 * done + 16 * k + 16)
                        sp.wait_ge(z_seg, k * NG + b * GPB + 1)
                        for part in range(len(PARTS)):
                            load_part(part, b)
                    sp.wait_ge(z_seg, k * NG + STEP_GROUPS + 1)
                    load_rest()
                with sp.Fori(1, NB) as d:
                    load_x(d)
                    with sp.If(d < NB - 1):
                        load_xT(d)

            def store(b):
                sp.dma_start(out_g[:, ds(b, 1), :, :].rearrange("p b q f -> p (b q) f"),
                             xc[:, ds(b * Q, Q), :]).then_inc(s_out, 16)

            with sp.Fori(0, NB - 1) as b:
                sp.wait_ge(s_yo, b + 1 + YS)
                store(b)
            sp.wait_ge(s_yo_full, 1)
            store(NB - 1)
            sp.wait_ge(s_out, 16 * NB)
            sp.wait_ge(s_out_last, 16)

        @block.gpsimd
        def _(pool):
            pool.memset(ident[:, :], 0.0).then_inc(s_const, 1)
            pool.memset(ones[:, :], 1.0).then_inc(s_const, 1)
            pool.memset(eps[:, :], EPS).then_inc(s_const, 1)
            pool.wait_ge(s_const, 1)
            pool.affine_select(out=ident[:, :], in_=ident[:, :], compare_op=ALU.not_equal, fill=1.0, base=0,
                               pattern=[[-1, P]], channel_multiplier=1).then_inc(s_const, 1)
            pool.iota(iota[:, :], pattern=[[1, NPB]], base=0, channel_multiplier=0,
                      allow_small_or_imprecise_dtypes=True).then_inc(s_iota, 1)
            pool.memset(vec_rows[:, :], 0.0).then_inc(s_vec0, 1)
            pool.memset(acc[:, :], 0.0).then_inc(s_acc0, 1)
            pool.memset(cnt_rows[:, :], 1.0).then_inc(s_cnt0, 1)

            def centre(d, src, n, q, n_x):
                pool.wait_ge(s_xm, d + 1)
                if n_x is not None:
                    pool.wait_ge(s_x, n_x)
                else:
                    pool.wait_ge(s_xl, 32)
                    pool.wait_ge(s_xc, d)
                mean = (x_mean if n_x is not None else x_mean_last)[0:n, 0:q].unsqueeze(2).broadcast_to([n, q, DX])
                pool.tensor_tensor(x_mid[0:n, 0:q, :], src, mean, ALU.subtract).then_inc(s_xmid, 1)
                pool.wait_ge(s_xmid, d + 1)
                pool.tensor_tensor(xc[0:n, ds(d * Q, q), :], x_mid[0:n, 0:q, :],
                                   b2c[0:n, :].unsqueeze(1).broadcast_to([n, q, DX]), ALU.add).then_inc(s_xc, 1)

            pool.wait_ge(s_b2c, 1)
            with pool.Fori(0, NB) as d:
                centre(d, x_blk[:, :, :], P, Q, 16 * d + 16)
            centre(NB, x_last[0:LAST_N, :].unsqueeze(1), LAST_N, 1, None)

            def scale(b, buf, n, q):
                pool.wait_ge(s_yrs, b + 1)
                rs = yrs[buf][0:n, 0:q].unsqueeze(2).broadcast_to([n, q, DX])
                pool.tensor_tensor(xc[0:n, ds(b * Q, q), :], y[buf][0:n, 0:q, :], rs, ALU.mult).then_inc(s_yo, 1)

            last_stage(pool, scale, NB - 1)

        @block.scalar
        def _(act):
            act.wait_ge(s_const, 3)
            act.activation(act_spare[:, :], eps[:, :], ACT.Sqrt).then_inc(s_table, 1)
            act.wait_ge(s_dst, 16)
            act.wait_ge(s_vec0, 1)
            act.dma_start(vec_rows[6:7, 0:DU], u[0:1, :]).then_inc(s_vec, 16)
            for k, vec in enumerate((b1, gamma, beta)):
                act.dma_start(vec_rows[2 * k:2 * k + 2, :], vec.rearrange("(j p) -> j p", j=2)).then_inc(s_vec, 16)
            act.dma_start(w1u[:, :], w1[DX + F:DX + F + DU, :]).then_inc(s_vec, 16)
            act.dma_start(w1x[:, :], w1[0:DX, :]).then_inc(s_w, 16)
            act.dma_start(w1e[:, :], w1[DX:DX + F, :]).then_inc(s_w, 16)
            act.dma_start(w2s[:, :, :], w2.rearrange("(j p) n -> p j n", j=2)).then_inc(s_w, 16)
            act.dma_start(b2s[:, :], b2.unsqueeze(0).broadcast_to([P, DX])).then_inc(s_w, 16)
            fl = on_flag(act)

            def mean_x(src, mean, junk):
                for k in range(src.shape[1]):
                    ins = act.activation(junk[0:src.shape[0], k, :], src[:, k, :], ACT.Identity, scale=1.0 / DX,
                                         accum_out=mean[:, k:k + 1])
                ins.then_inc(s_xm, 1)

            def hidden_out(count, j, src, at):
                act.wait_ge(s_h, count)
                act.activation(hT[:, j, at], src, ACT.Identity, bias=hb[:, j:j + 1]).then_inc(s_hs, 1)

            def dense(d, fast=False):
                act.wait_ge(s_x, 16 * d + 16)
                mean_x(x_blk[:, :, :], x_mean[:, :], x_junk[:, 0:Q, :])
                if fast:
                    act.wait_ge(s_acc, (d + 1) * GPB + MARGIN + GPB)
                for k in range(0, F, T):
                    ins = act.activation(cnt_rows[k:k + 1, :], acc[CNT:R, ds(d * NPB, NPB)], ACT.Identity)
                ins.then_inc(s_rowsc, 1)
                for j in range(2):
                    hidden_out(2 * d + j + 1, j, ps_h[j][:, :], ds(d * NPB, NPB))

            act.wait_ge(s_hbs, 1)
            act.wait_ge(s_cnt0, 1)
            with act.If(fl == 0):
                with act.Fori(0, NB - 1) as d:
                    dense(d, fast=True)
            with act.Else():
                act.wait_ge(z_fill, 1)
                with act.Fori(0, NB - 1) as d:
                    dense(d)
            d = NB - 1
            act.wait_ge(s_x, 16 * d + 16)
            mean_x(x_blk[:, :, :], x_mean[:, :], x_junk[:, 0:Q, :])
            act.wait_ge(s_xl, 32)
            mean_x(x_last[0:LAST_N, :].unsqueeze(1), x_mean_last[0:LAST_N, :], x_junk[:, Q:Q + 1, :])
            act.wait_ge(s_mT, 1)
            act.activation(meanT[:, :], ps_ft[0:F, :], ACT.Identity).then_inc(s_mTs, 1)
            for j in range(2):
                hidden_out(2 * d + j + 1, j, seg[j][:, 0:LAST_N], slice(NB * NPB, N))
            for j in range(2):
                hidden_out(2 * d + j + 3, j, ps_h[j][:, :], slice(d * NPB, NB * NPB))

            act.wait_ge(s_mv, 2)
            act.activation(sd[:, :], mv[:, :, 1], ACT.Sqrt, bias=eps[:, 0:1]).then_inc(s_sd, 1)

            def relu_and_root(b, buf, n, q):
                act.wait_ge(s_y, b + 1)
                for j in range(1 if isinstance(b, int) and b == 0 else 2):
                    act.activation(rT[buf][:, j, 0:n * q], hT[:, j, ds(b * NPB, n * q)], ACT.Relu,
                                   bias=bn_t[:, j:j + 1], scale=bn_s[:, j:j + 1]).then_inc(s_r, 1)
                lagging(b, buf, LAG_ROOT, root)

            def root(b, buf, n, q):
                act.wait_ge(s_sq, b + 1)
                act.activation(ysd[buf][0:n, 0:q], ssq[buf][0:n, 0:q], ACT.Sqrt, bias=eps[0:n, 0:1],
                               scale=1.0 / DX).then_inc(s_ysd, 1)

            act.wait_ge(s_bn, 5)
            last_stage(act, relu_and_root)
            flush(LAG_ROOT, root)
            buf = NB % YS
            act.wait_ge(s_yrs, NB + 1)
            act.activation(xc[0:LAST_N, NB * Q, :], y[buf][0:LAST_N, 0, :], ACT.Identity,
                           scale=yrs[buf][0:LAST_N, 0:1]).then_inc(s_yo_last, 1)
            act.wait_ge(s_yo_last, 1)
            act.dma_start(out[NB * NPB:N, :], xc[0:LAST_N, NB * Q, :]).then_inc(s_out_last, 16)

        @block.tensor
        def _(pe):
            def warm_up(n):
                for _ in range(n):
                    pe.matmul(ps_h[0][:, :], warm[:, 0:P], warm[:, :], start=True, stop=True)

            def sum_group(ps, rows, onehots, done):
                for s in range(SLOTS):
                    ins = pe.matmul(ps, rows[s], onehots[s], start=s == 0, stop=s == SLOTS - 1)
                ins.then_inc(done, 1)

            pe.wait_ge(s_warm, 1)
            warm_up(8)
            pe.wait_ge(s_const, 4)
            pe.wait_ge(s_base, 1)
            for t in range(2):
                ins = pe.matmul(ps_nm[:, t:NG:2], base[:, t:t + 1].broadcast_to([PAIRS, P]),
                                ident[0:PAIRS, 0:PAIRS], start=True, stop=True)
            ins.then_inc(s_rows, 1)
            warm_up(4)
            pe.wait_ge(s_bad, 1)
            pe.matmul(ps_ft[0:1, 0:2], ones[0:PAIRS, :], bad[:, 2, :], start=True, stop=True).then_inc(s_nbad, 1)

            def group(b, j):
                pe.wait_ge(s_oh, b * GPB + j + 1)
                pe.wait_ge(s_acc, b * GPB + earlier_user(j) + 1 + GPB)
                sum_group(seg[bank_of(j)][0:R, 0:W], ring_s[j], [onehot[:, j, s, :] for s in range(SLOTS)], s_seg)

            pe.wait_ge(s_edge[0], 16)
            for j in range(EARLY):
                group(0, j)
            fl = on_flag(pe)

            def transpose_vectors():
                pe.wait_ge(s_vec, 16 * 5)
                pe.transpose(ps_nm[:, 0:7], vec_rows[:, :], ident[0:7, 0:7]).then_inc(s_vecT, 1)

            def hidden_of_u():
                pe.wait_ge(s_w, 16 * 4)
                pe.wait_ge(s_vecs, 1)
                for j in range(2):
                    ins = pe.matmul(ps_nm[:, 8 + j:9 + j], w1u[:, j * P:(j + 1) * P], vecs[0:DU, 6:7],
                                    start=True, stop=True)
                ins.then_inc(s_hb, 1)

            def hidden_x(d, j, rows):
                pe.wait_ge(s_hs, 2 * d + j + 1)
                pe.matmul(ps_h[j][:, :], w1x[:, j * P:(j + 1) * P], rows, start=True, stop=False)

            def hidden_e(d, j):
                pe.wait_ge(s_mTs, d + 1)
                pe.matmul(ps_h[j][:, :], w1e[:, j * P:(j + 1) * P], meanT[:, :], start=False,
                          stop=True).then_inc(s_h, 1)

            def hidden(d, j):
                pe.wait_ge(s_xT, 16 * d + 16)
                hidden_x(d, j, xT[:, :])
                hidden_e(d, j)

            def last_hidden_x():
                pe.wait_ge(s_xl, 32)
                for j in range(2):
                    pe.matmul(seg[j][:, 0:LAST_N], w1x[:, j * P:(j + 1) * P], xT_end[:, NPB:], start=True, stop=False)

            def step(b, dense):
                starts = {a: k for k, (a, _) in enumerate(PARTS)}
                for j in range(0 if dense else EARLY, GPB):
                    if j in starts:
                        pe.wait_ge(s_edge[starts[j]], 16 * b + 16)
                    group(b, j)
                    if not dense:
                        if j == 12:
                            transpose_vectors()
                        if j == 15:
                            hidden_of_u()
                        continue
                    if j in AT_HIDDEN:
                        hidden(b - 1, AT_HIDDEN.index(j))

            with pe.If(fl == 0):
                step(0, False)
                with pe.Fori(1, NB) as b:
                    step(b, True)
                pe.wait_ge(s_edge[0], 16 * NB + 16)
                for j in range(REST):
                    group(NB, j)
                pe.wait_ge(s_acc, NB * GPB + 2 + GPB)
                last_hidden_x()
            with pe.Else():
                pe.wait_ge(s_dloc, 2)
                transpose_vectors()
                hidden_of_u()

                def slow_group(n, rows):
                    pe.wait_ge(z_oh, n + 1)
                    sum_group(seg[3][0:R, :], rows, [wide[:, s * NPB:(s + 1) * NPB] for s in range(SLOTS)], z_seg)

                with pe.Fori(0, NB + 1) as k:
                    with pe.Fori(0, NB) as b:
                        for part in range(1, len(PARTS)):
                            pe.wait_ge(s_edge[part], 16 * (k * NB + b) + 32)
                        pe.wait_ge(s_edge[0], 16 * (k * NB + b) + 16 * k + 32)
                        for j in range(GPB):
                            slow_group(k * NG + b * GPB + j, ring_s[j])
                    pe.wait_ge(s_edge[0], 16 * (k * NB + NB) + 16 * k + 32)
                    for j in range(REST):
                        slow_group(k * NG + STEP_GROUPS + j, ring_s[j])
                with pe.Fori(0, NB - 1) as d:
                    hidden(d, 0)
                    hidden(d, 1)
                pe.wait_ge(s_final, 1)
                last_hidden_x()
            d = NB - 1
            pe.wait_ge(s_final, 1)
            for k in range(Q):
                pe.transpose(ps_nm[:, k * R:(k + 1) * R], acc[:, d * NPB + k:NB * NPB:Q], ident[0:R, 0:R])
            pe.transpose(ps_nm[0:LAST_N, Q * R:(Q + 1) * R], acc[:, NB * NPB:N], ident[0:R, 0:R]).then_inc(s_nm, 1)
            hidden_x(d, 0, xT_end[:, 0:NPB])
            pe.wait_ge(s_mean, 1)
            for k in range(Q):
                ins = pe.transpose(ps_ft[0:F, k * P:(k + 1) * P], mean_nm[:, k, :], ident[:, :])
            ins.then_inc(s_mT, 1)
            pe.wait_ge(s_mean, 2)
            pe.transpose(seg[2][0:F, 0:LAST_N], mean_last[0:LAST_N, :], ident[0:LAST_N, 0:LAST_N]).then_inc(s_mTl, 1)
            hidden_x(d, 1, xT_end[:, 0:NPB])
            pe.wait_ge(s_mTls, 1)
            for j in range(2):
                pe.matmul(seg[j][:, 0:LAST_N], w1e[:, j * P:(j + 1) * P], meanT_last[:, :], start=False,
                          stop=True).then_inc(s_h, 1)
            for j in range(2):
                hidden_e(d, j)
            pe.wait_ge(s_hs, 2 * d + 5)
            warm_up(18)

            def second(b, buf, n, q):
                pe.wait_ge(s_r, 2 * b + 1)
                if isinstance(b, int) and b == 0:
                    pe.wait_ge(s_r0, 1)
                pe.wait_ge(s_ys, b + 1)
                for k in range(q):
                    for j in range(2):
                        ins = pe.matmul(seg[buf][0:n, k * DX:(k + 1) * DX], rT[buf][:, j, k * n:(k + 1) * n],
                                        w2c[:, j, :], start=j == 0, stop=j == 1)
                ins.then_inc(s_y, 1)

            pe.wait_ge(s_w2, 2)
            last_stage(pe, second)

        @block.vector
        def _(dve):
            pro = [0]

            def own(ins):
                pro[0] += 1
                ins.then_inc(s_pro, 1)
                dve.wait_ge(s_pro, pro[0])

            dve.memset(warm[:, :], 1.0).then_inc(s_warm, 1)
            dve.memset(spare[:, 9:10], 0.0).then_inc(s_hs, 2)
            dve.memset(spare[:, 0:1], 0.0).then_inc(s_acc, GPB)
            dve.wait_ge(s_dst, 16)
            dve.tensor_reduce(base[:, :], D[:, :, :].bitcast(mybir.dt.uint32), AX.X, ALU.min).then_inc(s_base, 1)
            dve.tensor_reduce(most[:, :], D[:, :, :], AX.X, ALU.max).then_inc(s_most, 1)

            def local_dst(a, z):
                dve.tensor_tensor(dloc[:, a:z, :], dcols[:, a:z, :],
                                  ps_nm[:, a:z].unsqueeze(2).broadcast_to([P, z - a, SLOTS]),
                                  ALU.subtract).then_inc(s_dloc, 1)

            def one_hot(b, j):
                group = b * GPB + j
                where = dloc[:, ds(group, 1), :].rearrange("p g s -> p (g s)").unsqueeze(2).broadcast_to([P, SLOTS, W])
                nodes = iota[:, 0:W].unsqueeze(1).broadcast_to([P, SLOTS, W])
                dve.tensor_tensor(onehot[:, j % GPB, :, :], nodes, where, ALU.is_equal).then_inc(s_oh, 1)

            dve.wait_ge(s_base, 1)
            dve.wait_ge(s_low, 16)
            dve.tensor_tensor(bad[:, 0, :], base[:, :], low[:, :], ALU.is_lt)
            dve.wait_ge(s_most, 1)
            own(dve.tensor_tensor(span[:, :], most[:, :], base[:, :], ALU.subtract))
            own(dve.tensor_scalar(bad[:, 1, :], span[:, :], float(W), None, ALU.is_ge))
            dve.scalar_tensor_tensor(bad[:, 1, :], base[:, :], float(N), bad[:, 1, :], ALU.is_ge,
                                     ALU.add).then_inc(s_most, 1)
            dve.wait_ge(s_rows, 1)
            dve.wait_ge(s_dcol, 16)
            local_dst(0, LEAD)
            dve.wait_ge(s_most, 2)
            dve.tensor_tensor(bad[:, 2, :], bad[:, 0, :], bad[:, 1, :], ALU.add).then_inc(s_bad, 1)
            dve.wait_ge(s_dloc, 1)
            dve.wait_ge(s_iota, 1)
            one_hot(0, 0)
            one_hot(0, 1)
            dve.wait_ge(s_nbad, 1)
            dve.tensor_reduce(x_mean[0:1, 0:1], ps_ft[0:1, 0:2], AX.X, ALU.add).then_inc(s_most, 1)
            dve.tensor_scalar(base_row[0:1, 0:NB, 0:GPB],
                              ps_nm[0:1, 0:STEP_GROUPS].rearrange("o (b g) -> o b g", g=GPB),
                              0.0, float(N - 1), ALU.max, ALU.min).then_inc(s_brow, 1)
            dve.wait_ge(s_most, 3)
            dve.tensor_scalar(flag[0:1, 0:1], x_mean[0:1, 0:1], 0.5, None, ALU.is_ge).then_inc(s_flag, 1)
            dve.tensor_scalar(base_row[0:1, NB, 0:REST], ps_nm[0:1, STEP_GROUPS:NG],
                              0.0, float(N - 1), ALU.max, ALU.min).then_inc(s_brow, 1)
            one_hot(0, 2)
            one_hot(0, 3)
            local_dst(LEAD, GPB + LEAD)
            dve.wait_ge(s_brow, 2)
            dve.wait_ge(s_dloc, 2)
            dve.wait_ge(s_acc0, 1)
            fl = on_flag(dve)

            def take_vectors():
                dve.wait_ge(s_vecT, 1)
                dve.tensor_copy(vecs[:, :], ps_nm[:, 0:7]).then_inc(s_vecs, 1)

            def hidden_constant():
                dve.wait_ge(s_vecs, 1)
                dve.wait_ge(s_hb, 1)
                dve.tensor_tensor(hb[:, :], ps_nm[:, 8:10], vecs[:, 0:2], ALU.add).then_inc(s_hbs, 1)

            def centre_weights():
                dve.wait_ge(s_w, 16 * 4)
                dve.tensor_reduce(b2m[:, :], b2s[:, :], AX.X, ALU.add).then_inc(s_small, 1)
                dve.tensor_reduce(w2m[:, :], w2s[:, :, :], AX.X, ALU.add).then_inc(s_small, 1)
                dve.wait_ge(s_small, 2)
                dve.tensor_scalar(b2m[:, :], b2m[:, :], 1.0 / DX, None, ALU.mult).then_inc(s_small, 1)
                dve.tensor_scalar(w2m[:, :], w2m[:, :], 1.0 / DX, None, ALU.mult).then_inc(s_small, 1)
                dve.wait_ge(s_small, 4)
                dve.tensor_scalar(b2c[:, :], b2s[:, :], b2m[:, 0:1], None, ALU.subtract).then_inc(s_b2c, 1)
                for j in range(2):
                    dve.tensor_scalar(w2c[:, j, :], w2s[:, j, :], w2m[:, j:j + 1], None,
                                      ALU.subtract).then_inc(s_w2, 1)

            def inverse(count, src, n, q, at):
                counts = src.rearrange("p (q f) -> p q f", f=R)[0:n, :, CNT]
                dve.tensor_scalar(cnt1[0:n, at:at + q], counts, 1.0, None, ALU.max).then_inc(s_cnt, 1)
                dve.wait_ge(s_cnt, count)
                dve.reciprocal(inv[0:n, at:at + q], cnt1[0:n, at:at + q]).then_inc(s_inv, 1)

            def means(count, dest, src, n, q, at):
                dve.wait_ge(s_inv, count)
                sums = src.rearrange("p (q f) -> p q f", f=R)[0:n, :, 0:F]
                dve.tensor_tensor(dest, sums, inv[0:n, at:at + q].unsqueeze(2).broadcast_to([n, q, F]),
                                  ALU.mult).then_inc(s_mean, 1)

            def block_inverse(d, part):
                if part == 0:
                    dve.wait_ge(s_rowsc, d + 1)
                    dve.transpose(cntT[:, :, :].rearrange("f c t -> f (c t)"), cnt_rows[:, :]).then_inc(s_cntT, 1)
                elif part == 1:
                    dve.wait_ge(s_cntT, d + 1)
                    dve.tensor_scalar(cntT_1[:, :], cntT[:, :, 0], 1.0, None, ALU.max).then_inc(s_cnt1, 1)
                    dve.wait_ge(s_cnt1, d + 1)
                    dve.reciprocal(cntT_inv[:, :], cntT_1[:, :]).then_inc(s_invT, 1)
                else:
                    dve.wait_ge(s_invT, d + 1)
                    dve.transpose(inv_rows[:, :].rearrange("f (c t) -> f c t", t=T),
                                  cntT_inv[:, :].unsqueeze(2).broadcast_to([F, NPB // T, T])).then_inc(s_inv_rows, 1)

            def block_means(d):
                dve.wait_ge(s_inv_rows, d + 1)
                dve.tensor_tensor(meanT[:, :].rearrange("f (q p) -> f q p", q=Q),
                                  acc[0:F, ds(d * NPB, NPB)].rearrange("f (p q) -> f q p", q=Q),
                                  inv_rows[:, :].rearrange("f (p q) -> f q p", q=Q), ALU.mult).then_inc(s_mTs, 1)

            def statistics(count, j, at, slot):
                dve.wait_ge(s_hs, count + 2)
                dve.bn_stats(stats[:, j, slot, :].rearrange("p b k -> p (b k)"), hT[:, j, at]).then_inc(s_st, 1)

            def block_statistics(d, j):
                statistics(2 * d + j + 1, j, ds(d * NPB, NPB), ds(d, 1))

            def bases(b, n):
                row = base_row[0:1, ds(b, 1), 0:n].rearrange("o b g -> o (b g)")
                _, vals = nc.values_load_multi_w_load_instructions(
                    row, engines=[mybir.EngineType.DVE], min_val=0, max_val=N - 1,
                    skip_runtime_bounds_check_because="base_row is clamped to these bounds when it is written")
                return vals

            def add_group(b, j, at, final=False):
                dve.wait_ge(s_seg, b * GPB + j + 1)
                dve.wait_ge(s_acc, b * GPB + j + GPB)
                window = acc[:, ds(at, W)]
                ins = dve.tensor_tensor(window, window, seg[bank_of(j)][0:R, 0:W], ALU.add)
                ins.then_inc(s_final if final else s_acc, 1)

            def step(b, dense):
                at = bases(b, GPB)
                for j in range(GPB):
                    one_hot(b, j + LEAD)
                    add_group(b, j, at[j])
                    if not dense:
                        if j == 2:
                            dve.wait_ge(s_dcol_rest, 16)
                            local_dst(GPB + LEAD, NG)
                        if j == 13:
                            dve.wait_ge(s_dloc, 3)
                            take_vectors()
                        continue
                    if j in AT_INVERSE:
                        block_inverse(b - 1, AT_INVERSE.index(j))
                    if j == AT_MEANS:
                        block_means(b - 1)
                    if j in AT_STATISTICS:
                        block_statistics(b - 1, AT_STATISTICS.index(j))

            with dve.If(fl == 0):
                step(0, False)
                hidden_constant()
                centre_weights()
                with dve.Fori(1, NB) as b:
                    step(b, True)
                at = bases(NB, REST)
                for j in range(REST):
                    add_group(NB, j, at[j], final=j == REST - 1)
            with dve.Else():
                dve.wait_ge(s_dcol_rest, 16)
                dve.tensor_copy(dloc[:, :, :], dcols[:, :, :]).then_inc(s_dloc, 1)
                take_vectors()
                hidden_constant()
                centre_weights()
                dve.wait_ge(s_dloc, 3)
                dve.wait_ge(s_seg, EARLY)
                flat = dloc[:, :, :].rearrange("p g s -> p (g s)")

                def slow_group(k, g):
                    n = k * NG + g
                    for s in range(SLOTS):
                        ins = dve.tensor_scalar(wide[:, s * NPB:(s + 1) * NPB], iota[:, :],
                                                flat[:, ds(g * SLOTS + s, 1)], None, ALU.is_equal)
                    ins.then_inc(z_oh, 1)
                    dve.wait_ge(z_seg, n + 2)
                    cols = acc[:, ds(k * NPB, NPB)]
                    dve.tensor_tensor(cols, cols, seg[3][0:R, :], ALU.add).then_inc(z_acc, 1)
                    dve.wait_ge(z_acc, n + 1)

                dve.memset(spare[:, 1:2], 0.0).then_inc(z_seg, 1)
                with dve.Fori(0, NB + 1) as k:
                    with dve.Fori(0, NG) as g:
                        slow_group(k, g)
                    dve.tensor_scalar(flat, flat, float(NPB), None, ALU.subtract).then_inc(z_sh, 1)
                    dve.wait_ge(z_sh, k + 1)
                dve.memset(spare[:, 2:3], 0.0).then_inc(z_fill, 1)
                with dve.Fori(0, NB - 1) as d:
                    for part in range(3):
                        block_inverse(d, part)
                    block_means(d)
                    block_statistics(d, 0)
                    block_statistics(d, 1)
                dve.memset(spare[:, 3:4], 0.0).then_inc(s_final, 1)
            d = NB - 1
            last = ps_nm[:, Q * R:(Q + 1) * R]
            dve.wait_ge(s_nm, 1)
            inverse(1, ps_nm[:, 0:Q * R], P, Q, 0)
            means(1, mean_nm[:, :, :], ps_nm[:, 0:Q * R], P, Q, 0)
            inverse(2, last, LAST_N, 1, Q)
            means(2, mean_last[0:LAST_N, :].unsqueeze(1), last, LAST_N, 1, Q)
            dve.wait_ge(s_mTl, 1)
            dve.tensor_copy(meanT_last[:, :], seg[2][0:F, 0:LAST_N]).then_inc(s_mTls, 1)
            for j in range(2):
                statistics(2 * d + j + 1, j, slice(NB * NPB, N), slice(NB, NB + 1))
            dve.memset(spare[:, 4:5], 0.0).then_inc(s_y, YS)
            dve.memset(spare[:, 5:6], 0.0).then_inc(s_ys, YS)
            dve.memset(spare[:, 6:7], 0.0).then_inc(s_yo, YS)
            statistics(2 * d + 3, 0, slice(d * NPB, NB * NPB), slice(d, NB))

            dve.wait_ge(s_st, 2 * NB + 1)
            dve.bn_aggr(mv[:, 0, :], stats[:, 0, :, :].rearrange("p b k -> p (b k)")).then_inc(s_mv, 1)
            statistics(2 * d + 4, 1, slice(d * NPB, NB * NPB), slice(d, NB))
            dve.wait_ge(s_st, 2 * NB + 2)
            dve.bn_aggr(mv[:, 1, :], stats[:, 1, :, :].rearrange("p b k -> p (b k)")).then_inc(s_mv, 1)
            dve.wait_ge(s_mv, 2)
            dve.tensor_scalar(bn_nm[:, :], mv[:, :, 0], -1.0, None, ALU.mult).then_inc(s_bn, 1)
            dve.wait_ge(s_sd, 1)
            dve.reciprocal(rsd[:, :], sd[:, :]).then_inc(s_bn, 1)
            dve.wait_ge(s_bn, 2)
            dve.tensor_tensor(bn_s[:, :], rsd[:, :], vecs[:, 2:4], ALU.mult).then_inc(s_bn, 1)
            dve.wait_ge(s_bn, 3)
            for j in range(2):
                dve.scalar_tensor_tensor(bn_t[:, j:j + 1], bn_nm[:, j:j + 1], bn_s[:, j:j + 1], vecs[:, 4 + j:5 + j],
                                         ALU.mult, ALU.add).then_inc(s_bn, 1)
            dve.wait_ge(s_bn, 5)
            dve.tensor_scalar(bn_h[:, :], hT[:, 1, 0:NPB], bn_s[:, 1:2], bn_t[:, 1:2], ALU.mult,
                              ALU.add).then_inc(s_bn, 1)
            dve.wait_ge(s_bn, 6)
            dve.tensor_scalar(rT[0][:, 1, :], bn_h[:, :], 0.0, None, ALU.max).then_inc(s_r0, 1)

            def finish(b, buf, n, q):
                dve.wait_ge(s_y, b + 1 + YS)
                dve.wait_ge(s_yo, b + 1)
                dve.tensor_tensor(y[buf][0:n, 0:q, :], seg[buf][0:n, 0:q * DX].rearrange("p (q f) -> p q f", q=q),
                                  xc[0:n, ds(b * Q, q), :], ALU.add).then_inc(s_ys, 1)
                lagging(b, buf, LAG_INV, inverse_sd)
                dve.wait_ge(s_ys, b + 1 + YS)
                for k in range(q):
                    ins = dve.tensor_tensor_reduce(
                        out=y_sq[buf][0:n, k, :], in0=y[buf][0:n, k, :], in1=y[buf][0:n, k, :], scale=1.0,
                        scalar=0.0, op0=ALU.mult, op1=ALU.add, accum_out=ssq[buf][0:n, k:k + 1])
                ins.then_inc(s_sq, 1)

            def inverse_sd(b, buf, n, q):
                dve.wait_ge(s_ysd, b + 1)
                dve.reciprocal(yrs[buf][0:n, 0:q], ysd[buf][0:n, 0:q]).then_inc(s_yrs, 1)

            dve.wait_ge(s_xc, NB + 1)
            last_stage(dve, finish)
            b, buf = NB - 1, (NB - 1) % YS
            inverse_sd(b, buf, P, Q)
            dve.wait_ge(s_yrs, NB)
            dve.tensor_tensor(xc[:, b * Q:(b + 1) * Q, :], y[buf][:, :, :],
                              yrs[buf][:, :].unsqueeze(2).broadcast_to([P, Q, DX]), ALU.mult).then_inc(s_yo_full, 1)
            inverse_sd(NB, NB % YS, LAST_N, 1)


def kernel(x, src, dst, edge_attr_96, L0_gnn_u, L0_gnn_W1, L0_gnn_b1, L0_gnn_gamma, L0_gnn_beta, L0_gnn_W2,
           L0_gnn_b2):
    import concourse.bacc as _bacc
    from concourse import mybir as _mybir
    from concourse.bass_utils import run_bass_kernel_spmd as _run

    edge, dst = np.asarray(edge_attr_96), np.asarray(dst)
    edge = np.pad(np.pad(edge, ((0, NG * GE - E), (0, 0))), ((0, 0), (0, 1)), constant_values=1)
    dst = np.pad(dst, (0, NG * GE - E), constant_values=-1)
    x = np.asarray(x)
    blocks = x[:NB * NPB].reshape(NB, P, Q, DX).transpose(3, 0, 2, 1).reshape(DX, NB * NPB)
    xt = np.concatenate([blocks, x[NB * NPB:].T], axis=1)

    nc = _bacc.Bacc("TRN2", target_bir_lowering=False, num_devices=1)
    arrays, args = {}, []
    for name, a in (("x", x), ("xt", xt), ("dst_rows", dst.reshape(PAIRS, 2, GE)),
                    ("dst_cols", dst.reshape(NG, P, SLOTS).transpose(1, 0, 2)), ("edge", edge),
                    ("u", L0_gnn_u), ("w1", L0_gnn_W1), ("b1", L0_gnn_b1), ("gamma", L0_gnn_gamma),
                    ("beta", L0_gnn_beta), ("w2", L0_gnn_W2), ("b2", L0_gnn_b2), ("lowest", lower_bounds())):
        a = np.ascontiguousarray(a)
        arrays[f"in_{name}"] = a
        args.append(nc.dram_tensor(f"in_{name}", a.shape, _mybir.dt.from_np(a.dtype), kind="ExternalInput").ap())
    args.append(nc.dram_tensor("out_0", (N, DX), _mybir.dt.float32, kind="ExternalOutput").ap())
    gnn_kernel(nc, *args)
    r = _run(nc, [arrays], core_ids=[0])
    return r.results[0]["out_0"]
```
